# Optimizing a Trainium2 kernel written in Bass

```python
import numpy as np
import jax
import jax.numpy as jnp

def _softmax(x, axis=-1):
    return jax.nn.softmax(x, axis=axis)

def _gelu(x):
    return jax.nn.gelu(x, approximate=True)

def _silu(x):
    return jax.nn.silu(x)

def _sigmoid(x):
    return jax.nn.sigmoid(x)

def _layernorm(x, axis=-1, eps=1e-05):
    m = jnp.mean(x, axis=axis, keepdims=True)
    v = jnp.var(x, axis=axis, keepdims=True)
    return (x - m) / jnp.sqrt(v + eps)

def _scatter_add(tgt, idx, src, axis=0):
    return tgt.at[idx].add(src)

def _segment_sum(src, seg, n):
    return jax.ops.segment_sum(src, seg, n)
kernel_name = 'mk_adj_resnorm_d2_adj_r2_b85815'

def setup_inputs(seed: int=0):
    np.random.seed(seed)
    _w = jnp.asarray

    def _rec_inputs():
        import jax
        import jax.numpy as jnp
        _gk = jax.random.key(seed)
        x = -0.0005207 + 1.001 * jax.random.normal(jax.random.fold_in(_gk, 1), (8192, 128), jnp.float32)
        _w = (1.0 + jnp.arange(8192, dtype=jnp.float32)) ** (-0.5)
        _w = _w / _w.mean()
        _pij = jnp.clip(0.00195312 * _w[:, None] * _w[None, :], 0.0, 1.0)
        _a = jax.random.uniform(jax.random.fold_in(_gk, 2), (8192, 8192)) < _pij
        _a = jnp.logical_or(_a, jnp.eye(8192, dtype=bool))
        _af = _a.astype(jnp.float32)
        adj = _af
        return (x, adj)
    x, adj = _rec_inputs()

    def _L0_gnn_setup():
        import jax, jax.numpy as jnp
        import numpy as np
        N = 4096
        E = 4096
        C = 128
        ALPHA = 0.1
        BETA = 0.5
        key = jax.random.key(seed)
        k1, k2, k3 = jax.random.split(key, 3)
        x_0 = jax.random.normal(k1, (N, C), dtype=jnp.float32)
        mask = (jax.random.uniform(k2, (N, E)) < 0.004).astype(jnp.float32)
        idx = jnp.arange(N)
        incidence_1 = mask.at[idx, idx].set(1.0)
        W = jax.random.normal(k3, (C, C), dtype=jnp.float32) / jnp.sqrt(C)
        return {'x_0': x_0, 'incidence_1': incidence_1, 'W': W}
    _L0_gnn_all = _L0_gnn_setup()
    _L0_gnn_in = {k: v for k, v in _L0_gnn_all.items() if k in ('W',)}
    del _L0_gnn_all

    def _L1_gnn_setup():
        import jax, jax.numpy as jnp
        import numpy as np
        MIN_NORM = 1e-15
        BALL_EPS = 1e-05
        C_IN = 1.0
        C_OUT = 1.0

        def _artanh(x):
            x = jnp.clip(x, -1.0 + 1e-07, 1.0 - 1e-07)
            return 0.5 * (jnp.log1p(x) - jnp.log1p(-x))

        def _norm(x):
            return jnp.maximum(jnp.linalg.norm(x, axis=-1, keepdims=True), MIN_NORM)

        def proj(x, c):
            norm = _norm(x)
            maxnorm = (1.0 - BALL_EPS) / jnp.sqrt(c)
            return jnp.where(norm > maxnorm, x / norm * maxnorm, x)

        def expmap0(u, c):
            sc = jnp.sqrt(c)
            un = _norm(u)
            return jnp.tanh(sc * un) * u / (sc * un)

        def logmap0(p, c):
            sc = jnp.sqrt(c)
            pn = _norm(p)
            return _artanh(sc * pn) * p / (sc * pn)

        def mobius_matvec(m, x, c):
            sc = jnp.sqrt(c)
            xn = _norm(x)
            mx = x @ m.T
            mxn = _norm(mx)
            res = jnp.tanh(mxn / xn * _artanh(sc * xn)) * mx / (mxn * sc)
            zero_row = jnp.all(mx == 0, axis=-1, keepdims=True)
            return jnp.where(zero_row, jnp.zeros((), dtype=res.dtype), res)

        def mobius_add(x, y, c):
            x2 = jnp.sum(x * x, axis=-1, keepdims=True)
            y2 = jnp.sum(y * y, axis=-1, keepdims=True)
            xy = jnp.sum(x * y, axis=-1, keepdims=True)
            num = (1.0 + 2.0 * c * xy + c * y2) * x + (1.0 - c * x2) * y
            denom = 1.0 + 2.0 * c * xy + c * c * x2 * y2
            return num / jnp.maximum(denom, MIN_NORM)
        key = jax.random.key(seed)
        k1, k2, k3, k4 = jax.random.split(key, 4)
        N, D_IN, D_OUT = (4096, 128, 128)
        x = proj(0.05 * jax.random.normal(k1, (N, D_IN), dtype=jnp.float32), C_IN)
        adj = jax.random.uniform(k2, (N, N), dtype=jnp.float32)
        adj = adj / jnp.sum(adj, axis=1, keepdims=True)
        bound = np.sqrt(2.0) * np.sqrt(6.0 / (D_IN + D_OUT))
        weight = jax.random.uniform(k3, (D_OUT, D_IN), dtype=jnp.float32, minval=-bound, maxval=bound)
        bias = 0.01 * jax.random.normal(k4, (D_OUT,), dtype=jnp.float32)
        return {'x': x, 'adj': adj, 'weight': weight, 'bias': bias}
    _L1_gnn_all = _L1_gnn_setup()
    _L1_gnn_in = {k: v for k, v in _L1_gnn_all.items() if k in ('weight', 'bias')}
    del _L1_gnn_all
    return {'x': x, 'adj': adj, 'L0_gnn_W': _L0_gnn_in['W'], 'L1_gnn_weight': _L1_gnn_in['weight'], 'L1_gnn_bias': _L1_gnn_in['bias']}

def reference(x, adj, L0_gnn_W, L1_gnn_weight, L1_gnn_bias):
    import jax
    import jax.numpy as jnp

    def _L0_gnn_ref(x_0, incidence_1, W):
        import jax, jax.numpy as jnp
        import numpy as np
        N = 4096
        E = 4096
        C = 128
        ALPHA = 0.1
        BETA = 0.5
        m_0_1 = incidence_1.T @ x_0
        node_degree = jnp.sum(incidence_1, axis=1)
        edge_degree = node_degree @ incidence_1 / jnp.sum(incidence_1, axis=0)
        m_1_0 = incidence_1 @ (m_0_1 / jnp.sqrt(edge_degree)[:, None]) / jnp.sqrt(node_degree)[:, None]
        x_combined = (1.0 - ALPHA) * m_1_0 + ALPHA * x_0
        return (1.0 - BETA) * x_combined + BETA * (x_combined @ W.T)

    def _L1_gnn_ref(x, adj, weight, bias):
        import jax, jax.numpy as jnp
        import numpy as np
        MIN_NORM = 1e-15
        BALL_EPS = 1e-05
        C_IN = 1.0
        C_OUT = 1.0

        def _artanh(x):
            x = jnp.clip(x, -1.0 + 1e-07, 1.0 - 1e-07)
            return 0.5 * (jnp.log1p(x) - jnp.log1p(-x))

        def _norm(x):
            return jnp.maximum(jnp.linalg.norm(x, axis=-1, keepdims=True), MIN_NORM)

        def proj(x, c):
            norm = _norm(x)
            maxnorm = (1.0 - BALL_EPS) / jnp.sqrt(c)
            return jnp.where(norm > maxnorm, x / norm * maxnorm, x)

        def expmap0(u, c):
            sc = jnp.sqrt(c)
            un = _norm(u)
            return jnp.tanh(sc * un) * u / (sc * un)

        def logmap0(p, c):
            sc = jnp.sqrt(c)
            pn = _norm(p)
            return _artanh(sc * pn) * p / (sc * pn)

        def mobius_matvec(m, x, c):
            sc = jnp.sqrt(c)
            xn = _norm(x)
            mx = x @ m.T
            mxn = _norm(mx)
            res = jnp.tanh(mxn / xn * _artanh(sc * xn)) * mx / (mxn * sc)
            zero_row = jnp.all(mx == 0, axis=-1, keepdims=True)
            return jnp.where(zero_row, jnp.zeros((), dtype=res.dtype), res)

        def mobius_add(x, y, c):
            x2 = jnp.sum(x * x, axis=-1, keepdims=True)
            y2 = jnp.sum(y * y, axis=-1, keepdims=True)
            xy = jnp.sum(x * y, axis=-1, keepdims=True)
            num = (1.0 + 2.0 * c * xy + c * y2) * x + (1.0 - c * x2) * y
            denom = 1.0 + 2.0 * c * xy + c * c * x2 * y2
            return num / jnp.maximum(denom, MIN_NORM)
        h = proj(mobius_matvec(weight, x, C_IN), C_IN)
        hyp_bias = proj(expmap0(bias[None, :], C_IN), C_IN)
        h = proj(mobius_add(h, hyp_bias, C_IN), C_IN)
        x_tangent = logmap0(h, C_IN)
        support_t = adj @ x_tangent
        h = proj(expmap0(support_t, C_IN), C_IN)
        xt = jax.nn.relu(logmap0(h, C_IN))
        return proj(expmap0(xt, C_OUT), C_OUT)
    x = _layernorm(x + _L0_gnn_ref(x, adj, L0_gnn_W), axis=-1)
    x = _layernorm(x + _L1_gnn_ref(x, adj, L1_gnn_weight, L1_gnn_bias), axis=-1)
    return x

_drawn_inputs = setup_inputs


def setup_inputs(seed=0):
    import zlib

    import numpy as np

    out = dict(_drawn_inputs(seed))
    spreads = {}
    factors = {}
    for name, (base, spread) in spreads.items():
        noise = np.random.default_rng([zlib.crc32(name.encode()), seed]).standard_normal(out[name].shape)
        drawn = base * np.exp(spread * noise) if base else spread * noise
        out[name] = jnp.asarray(drawn.astype(out[name].dtype))
    for name, factor in factors.items():
        out[name] = (out[name] * factor).astype(out[name].dtype)
    return out
```

```python
from contextlib import ExitStack

import concourse.bass as bass
from concourse import mybir

P = 128
N = 8192
C = 128
NB = N // P
PARTS = 3
CHUNK = 2048
NCH = N // CHUNK
GROUP = 4
NG = NB // GROUP
PANEL = 1024
NP = N // PANEL
PB = PANEL // P
BANK = 512
BITS = 8
NQ = NB // BITS

ALPHA, BETA = 0.1, 0.5
LN_EPS = 1e-5
MIN_NORM = 1e-15
MIN_SQ = 1e-30
MAX_NORM = 1.0 - 1e-5
ATANH_CLIP = 1.0 - 1e-7
TWO = 2.0
BIT = 0x40404040

ALU = mybir.AluOpType
ACT = mybir.ActivationFunctionType
AX = mybir.AxisListType.X
F32 = mybir.dt.float32
BF16 = mybir.dt.bfloat16
F8 = mybir.dt.float8e4
U8 = mybir.dt.uint8
U32 = mybir.dt.uint32

ATANH = ["one_minus", "inv_one_minus", "v", "u", "u_minus_1", "is_one", "log_fixed", "denominator",
         "inv_denominator", "ratio", "atanh"]
E1_DVE = ["scaled", "with_x", "row_sum", "mean", "centered",
          "square_sum", "variance", "inv_std", "x1",
          "x_sq", "mx_sq", "bias_product", "dot", "floor_x", "floor_mx", "clip_x",
          *["x_" + s for s in ATANH],
          "inv_xn", "ratio_norms", "tanh_arg", "t_clipped", "inv_mxn", "a", "aa", "x2", "xy2",
          "x2y2", "den", "den_floor", "inv_den", "num", "num_a", "A", "one_minus_x2", "B",
          "h_part", "b_part", "h2", "h_sq", "floor_h", "clip_h",
          *["h_" + s for s in ATANH],
          "inv_n2", "kappa", "xt", "rest1", "rest2"]
E1_ACT = ["mT", "centered_sq", "std", "x1T", "x1_squares", "mx_squares", "xn", "mxn",
          "x_log", "tanh", "h_squares", "n2", "h_log", "part0", "part1", "part2"]
E2_DVE = ["relu", "s_sq", "r_sq", "floor_s", "th_clipped",
          *["s_" + s for s in ATANH],
          "inv_un", "kappa", "kk", "w_sq", "floor_w", "tw_clipped", "inv_wn", "kt", "kappa2",
          "scaled", "with_x1", "row_sum", "mean", "centered",
          "square_sum", "variance", "inv_std", "out"]
E2_ACT = ["sT", "s_squares", "r_squares", "un", "th", "s_log", "wn", "tw", "centered_sq", "std"]


def step_value(steps, round_, name):
    return round_ * len(steps) + steps.index(name) + 1


def build(nc, x, adj, W0, W1, bias, out, x1_dram):
    with ExitStack() as ctx:
        def sb(name, shape, dt):
            return ctx.enter_context(nc.sbuf_tensor(name, shape, dt))

        def sem(name):
            return ctx.enter_context(nc.semaphore(name))

        work = sb("work", [P, 96 * 1024], U8)
        adj_in = work[:, 0:32768].bitcast(F32).rearrange("p (s n) -> p s n", s=NCH)
        adj8 = work[:, 32768:98304].bitcast(F8).rearrange("p (g u n) -> p g u n", g=2, u=GROUP)
        split_bytes = PARTS * NB * C * 2
        y_parts = work[:, 0:split_bytes].bitcast(BF16).rearrange("p (s b c) -> p s b c", s=PARTS, b=NB)
        xt_parts = work[:, split_bytes:2 * split_bytes].bitcast(BF16).rearrange("p (s b c) -> p s b c", s=PARTS, b=NB)
        y_full = work[:, split_bytes:split_bytes + 8192].bitcast(F32).rearrange("p (s n) -> p s n", s=2)
        y_rest = work[:, split_bytes + 8192:split_bytes + 24576].bitcast(F32).rearrange("p (s n) -> p s n", s=4)
        adjT = sb("adjT", [P, NQ, N], U8)
        acc_space = sb("acc_space", [P, N], F32)
        rows = [acc_space[:, i * PANEL:(i + 1) * PANEL].rearrange("p (b c) -> p b c", b=PB) for i in range(8)]
        x_rows, x_scaled, colT, x1_rows, centered, squares, h_rows, spare = rows
        slots_space = sb("slots", [P, BITS * PANEL], U8)
        plane = slots_space[:, :].rearrange("p (k n) -> p k n", k=BITS)
        packed = slots_space[:, 0:1024]
        packed16 = slots_space[:, 1024:3072].bitcast(BF16)
        sink = slots_space[:, 3072:3072 + CHUNK]
        x_in = slots_space[:, 5120:7168].bitcast(F32).rearrange("p (u c) -> p u c", u=GROUP)
        small = sb("small", [P, 2 * GROUP * PARTS * C], BF16)
        x_parts = small[:, :].rearrange("p (g s u c) -> p g s u c", g=2, s=PARTS, u=GROUP)
        stats = small[:, :].bitcast(F32)
        ident = sb("ident", [P, P], F32)
        ident16 = sb("ident16", [P, P], BF16)
        degree = sb("degree", [P, NB], F32)
        row_counts = sb("row_counts", [P, 2, NCH], F32)
        sum_parts = sb("sum_parts", [P, 2, 4], BF16)
        bias_stats = sb("bias_stats", [P, 24], F32)

        ps = [ctx.enter_context(nc.psum_tensor(f"ps{i}", [P, PANEL], F32)) for i in range(4)]
        panel_ps = ps[0:2]
        sums_ps = ps[2][:, 0:3 * NB].rearrange("p (b v) -> p b v", b=NB)
        packed_ps = ps[2][:, BANK:2 * BANK].bitcast(BF16).rearrange("p (q i) -> p q i", q=NQ)
        weights_ps = ps[3]
        turn_ps = ps[0:2]
        acc = ps[2]
        mm_ps, tr_ps = ps[0], ps[1]

        s_adj = [sem(f"adj_loaded{i}") for i in range(NCH)]
        s_x = sem("x_loaded")
        s_const = sem("constants_loaded")
        s_ident = sem("identity_ready")
        s_wT = sem("weights_turned")
        s_prep = sem("weights_ready")
        s_bias = sem("bias_steps")
        s_bias_act = sem("bias_act")
        s_bias_done = sem("bias_ready")
        s_counted = sem("chunks_counted")
        s_conv = sem("chunks_converted")
        s_pack = sem("pack_steps")
        s_packed = sem("units_packed")
        s_packed16 = sem("units_widened")
        s_turned = sem("units_turned")
        s_stored = sem("units_stored")
        s_summed = sem("rows_summed")
        s_rs = sem("row_sum_steps")
        s_rs_ready = sem("row_sums_ready")
        s_rs_used = sem("row_sums_used")
        s_xs_steps = sem("x_split_steps")
        s_xs = sem("x_split")
        s_apart = sem("waits_apart")
        s_panel = sem("panels_multiplied")
        s_added = sem("panels_added")
        s_edge = sem("edge_steps")
        s_edge_act = sem("edge_act")
        s_yturn = sem("y_turned")
        s_ydve = sem("y_dve")
        s_yact = sem("y_act")
        s_plane = sem("planes_unpacked")
        s_used = sem("planes_used")
        s_acc = sem("panels_contracted")
        s_xrows = sem("x_rows_loaded")
        s_xsc = sem("x_scaled")
        s_e1d = sem("epilogue1_dve")
        s_e1a = sem("epilogue1_act")
        s_s1 = sem("epilogue1_combined")
        s_s2 = sem("epilogue1_turned")
        s_s3 = sem("epilogue1_mapped")
        s_x1out = sem("x1_stored")
        s_x1in = sem("x1_loaded")
        s_e2d = sem("epilogue2_dve")
        s_e2a = sem("epilogue2_act")
        s_e2t = sem("epilogue2_turned")
        s_out = sem("out_stored")

        adj_rows = adj.rearrange("(b p) n -> b p n", p=P)
        x_groups = x.rearrange("(g u p) c -> g p u c", u=GROUP, p=P)
        x_panels = x.rearrange("(t b p) c -> t p b c", b=PB, p=P)
        x1_panels = x1_dram.rearrange("(t b p) c -> t p b c", b=PB, p=P)
        out_panels = out.rearrange("(t b p) c -> t p b c", b=PB, p=P)

        def wide(v):
            return v.unsqueeze(2).to_broadcast([P, PB, C])

        edge_ratio, edge_root, y_scale, degree_root, node_scale = [
            stats[:, i * NB:(i + 1) * NB] for i in range(5)]
        weights = stats[:, 5 * NB:5 * NB + 5 * C].rearrange("p (i c) -> p i c", i=5)
        w_in, V, W1T, hyp_bias = weights[:, 0:2], weights[:, 2], weights[:, 3], weights[:, 4]
        row_values = stats[:, 5 * NB + 5 * C:]

        class Row:

            def __init__(self, base):
                self.base, self.at = base, {}

            def __getitem__(self, name):
                i = self.base + self.at.setdefault(name, len(self.at))
                assert (i + 1) * PB <= row_values.shape[1]
                return row_values[:, i * PB:(i + 1) * PB]

        val1, val2 = Row(0), Row(0)
        mm_blocks = mm_ps[:, :].rearrange("p (b c) -> p b c", b=PB)
        tr_blocks = tr_ps[:, :].rearrange("p (b c) -> p b c", b=PB)
        acc_blocks = acc[:, :].rearrange("p (b c) -> p b c", b=PB)
        adjT32 = adjT[:, :, :].bitcast(U32)
        plane32 = plane[:, :, :].bitcast(U32)

        def apart(eng):
            eng.sem_inc(s_apart, 1)

        block = ctx.enter_context(nc.Block())

        @block.sync
        def _(sp):

            def load_row_block(r, first):
                for c in range(NCH):
                    if not first:
                        sp.wait_ge(s_counted, r * NCH + c - NCH + 1)
                        sp.wait_ge(s_conv, r * NCH + c - NCH + 1)
                    sp.dma_start(adj_in[:, c, :], adj_rows[r, :, c * CHUNK:(c + 1) * CHUNK]).then_inc(s_adj[c], 16)

            def load_x_group(g, first):
                if not first:
                    sp.wait_ge(s_xs, g)
                sp.dma_start(x_in[:, :, :], x_groups[g]).then_inc(s_x, 16)

            load_row_block(0, True)
            load_x_group(0, True)
            for u in range(1, GROUP):
                load_row_block(u, False)
            with sp.Fori(1, NG) as g:
                load_x_group(g, False)
                for u in range(GROUP):
                    load_row_block(g * GROUP + u, False)

            sp.wait_ge(s_panel, NG * NP)
            sp.dma_start(w_in[:, 0, :], W0).then_inc(s_const, 16)
            sp.dma_start(w_in[:, 1, :], W1).then_inc(s_const, 16)
            sp.dma_start(hyp_bias, bias.unsqueeze(0).to_broadcast([P, C])).then_inc(s_const, 16)

            def x_panel(t, first):
                if first:
                    sp.wait_ge(s_yturn, NP)
                else:
                    sp.wait_ge(s_e1d, step_value(E1_DVE, t - 1, "with_x"))
                    sp.wait_ge(s_xsc, t)
                sp.dma_start(x_rows, x_panels[t]).then_inc(s_xrows, 16)

            def x1_store(e):
                sp.wait_ge(s_e1d, step_value(E1_DVE, e, "x1"))
                sp.dma_start(x1_panels[e], x1_rows).then_inc(s_x1out, 16)

            x_panel(0, True)
            with sp.Fori(1, NP) as t:
                x_panel(t, False)
                x1_store(t - 1)
            x1_store(NP - 1)
            sp.wait_ge(s_x1out, 16 * NP)

            def x1_load(e, first):
                if not first:
                    sp.wait_ge(s_e2d, step_value(E2_DVE, e - 1, "with_x1"))
                sp.dma_start(x_rows, x1_panels[e]).then_inc(s_x1in, 16)

            def out_store(e):
                sp.wait_ge(s_e2d, step_value(E2_DVE, e, "out"))
                sp.dma_start(out_panels[e], x1_rows).then_inc(s_out, 16)

            x1_load(0, True)
            with sp.Fori(1, NP) as e:
                out_store(e - 1)
                x1_load(e, False)
            out_store(NP - 1)
            sp.wait_ge(s_out, 16 * NP)

        @block.gpsimd
        def _(pool):
            nc.gpsimd.memset(ident[:, :], 0.0).then_inc(s_ident, 1)
            pool.wait_ge(s_ident, 1)
            nc.gpsimd.affine_select(out=ident[:, :], in_=ident[:, :], compare_op=ALU.not_equal, fill=1.0,
                                    base=0, pattern=[[-1, P]], channel_multiplier=1).then_inc(s_ident, 1)
            pool.wait_ge(s_ident, 2)
            nc.gpsimd.tensor_copy(ident16[:, :], ident[:, :]).then_inc(s_ident, 1)
            nc.gpsimd.memset(sum_parts[:, :, :], 1.0).then_inc(s_ident, 1)

            def split_x(g, parity, early):
                pool.wait_ge(s_x, 16 * (g + 1))
                if not early:
                    pool.wait_ge(s_panel, (g - 1) * NP)
                apart(pool)
                part = x_parts[:, parity]
                nc.gpsimd.tensor_copy(part[:, 0], x_in[:, :, :]).then_inc(s_xs_steps, 1)
                pool.wait_ge(s_xs_steps, g * 4 + 1)
                apart(pool)
                nc.gpsimd.tensor_tensor(x_in[:, :, :], x_in[:, :, :], part[:, 0], ALU.subtract).then_inc(s_xs_steps, 1)
                pool.wait_ge(s_xs_steps, g * 4 + 2)
                apart(pool)
                nc.gpsimd.tensor_copy(part[:, 1], x_in[:, :, :]).then_inc(s_xs_steps, 1)
                pool.wait_ge(s_xs_steps, g * 4 + 3)
                apart(pool)
                nc.gpsimd.tensor_tensor(x_in[:, :, :], x_in[:, :, :], part[:, 1], ALU.subtract).then_inc(s_xs_steps, 1)
                pool.wait_ge(s_xs_steps, g * 4 + 4)
                apart(pool)
                nc.gpsimd.tensor_copy(part[:, 2], x_in[:, :, :]).then_inc(s_xs, 1)

            def widen(g, u):
                r = g * GROUP + u
                pool.wait_ge(s_packed, r + 1)
                apart(pool)
                nc.gpsimd.tensor_copy(packed16, packed).then_inc(s_packed16, 1)

            def group(g, parity, early=False, first=False):
                split_x(g, parity, early)
                for u in range(GROUP):
                    if not (first and u == 0):
                        pool.wait_ge(s_turned, g * GROUP + u)
                    widen(g, u)

            group(0, 0, early=True, first=True)
            group(1, 1, early=True)
            with pool.Fori(1, NG // 2) as pair:
                group(2 * pair, 0)
                group(2 * pair + 1, 1)

        @block.scalar
        def _(act):
            def count(r, parity):
                for c in range(NCH):
                    act.wait_ge(s_adj[c], 16 * (r + 1))
                    act.wait_ge(s_counted, r * NCH + c)
                    nc.scalar.activation(sink, adj_in[:, c, :].bitcast(U32), ACT.Sign,
                                         accum_out=row_counts[:, parity, c:c + 1]).then_inc(s_counted, 1)

            def store(r):
                act.wait_ge(s_turned, r + 1)
                nc.scalar.activation(adjT[:, :, bass.ds(r * P, P)], packed_ps, ACT.Copy).then_inc(s_stored, 1)

            count(0, 0)
            for u in range(1, GROUP):
                if u >= 2:
                    act.wait_ge(s_summed, u - 1)
                count(u, u % 2)
                store(u - 1)
            with act.Fori(1, NG) as g:
                for u in range(GROUP):
                    r = g * GROUP + u
                    act.wait_ge(s_summed, r - 1)
                    count(r, u % 2)
                    store(r - 1)
            store(NB - 1)

            act.wait_ge(s_edge, 4)
            nc.scalar.activation(edge_root, edge_ratio, ACT.Sqrt).then_inc(s_edge_act, 1)
            nc.scalar.activation(degree_root, degree[:, :], ACT.Sqrt).then_inc(s_edge_act, 1)
            for b in range(NP):
                sl = slice(b * PB, (b + 1) * PB)
                act.wait_ge(s_ydve, 3 * b + 1)
                nc.scalar.activation(y_parts[:, 0, sl, :], y_full[:, b % 2, :].rearrange("p (b c) -> p b c", b=PB),
                                     ACT.Copy).then_inc(s_yact, 1)
                act.wait_ge(s_ydve, 3 * b + 2)
                nc.scalar.activation(y_parts[:, 1, sl, :], y_rest[:, 2 * (b % 2), :].rearrange("p (b c) -> p b c", b=PB),
                                     ACT.Copy).then_inc(s_yact, 1)
                act.wait_ge(s_ydve, 3 * b + 3)
                nc.scalar.activation(y_parts[:, 2, sl, :], y_rest[:, 2 * (b % 2) + 1, :].rearrange("p (b c) -> p b c", b=PB),
                                     ACT.Copy).then_inc(s_yact, 1)

            act.wait_ge(s_bias, 3)
            nc.scalar.activation(bias_stats[:, 2:3], bias_stats[:, 1:2], ACT.Sqrt).then_inc(s_bias_act, 1)
            act.wait_ge(s_bias_act, 1)
            nc.scalar.activation(bias_stats[:, 3:4], bias_stats[:, 2:3], ACT.Tanh).then_inc(s_bias_act, 1)

            def epilogue1(e, first=False):
                def after_dve(name):
                    act.wait_ge(s_e1d, step_value(E1_DVE, e, name))

                order = iter(E1_ACT)

                def did(name, ins):
                    assert next(order) == name
                    ins.then_inc(s_e1a, 1)

                v = val1
                act.wait_ge(s_acc, e + 1)
                if not first:
                    act.wait_ge(s_s3, e)
                did("mT", nc.scalar.copy(colT, acc_blocks))
                after_dve("centered")
                did("centered_sq", nc.scalar.activation(squares, centered, ACT.Square))
                after_dve("variance")
                did("std", nc.scalar.activation(v["std"], v["variance"], ACT.Sqrt))
                act.wait_ge(s_s2, e + 1)
                did("x1T", nc.scalar.copy(colT, tr_blocks))
                did("x1_squares", nc.scalar.activation(squares, x1_rows, ACT.Square))
                act.wait_ge(s_s3, e + 1)
                did("mx_squares", nc.scalar.activation(h_rows, mm_blocks, ACT.Square))
                after_dve("floor_mx")
                did("xn", nc.scalar.activation(v["xn"], v["x_sq"], ACT.Sqrt))
                did("mxn", nc.scalar.activation(v["mxn"], v["mx_sq"], ACT.Sqrt))
                after_dve("x_u")
                did("x_log", nc.scalar.activation(v["log"], v["u"], ACT.Ln))
                after_dve("tanh_arg")
                did("tanh", nc.scalar.activation(v["t"], v["tanh_arg"], ACT.Tanh))
                after_dve("h2")
                did("h_squares", nc.scalar.activation(squares, h_rows, ACT.Square))
                after_dve("floor_h")
                did("n2", nc.scalar.activation(v["n2"], v["h_sq"], ACT.Sqrt))
                after_dve("h_u")
                did("h_log", nc.scalar.activation(v["log"], v["u"], ACT.Ln))
                for k, name in enumerate(["xt", "rest1", "rest2"]):
                    after_dve(name)
                    dst = xt_parts[:, k, bass.ds(e * PB, PB), :]
                    did(f"part{k}", nc.scalar.activation(dst, [h_rows, spare, squares][k], ACT.Copy))

            def epilogue2(e, first=False):
                def after_dve(name):
                    act.wait_ge(s_e2d, step_value(E2_DVE, e, name))

                order = iter(E2_ACT)

                def did(name, ins):
                    assert next(order) == name
                    ins.then_inc(s_e2a, 1)

                v = val2
                act.wait_ge(s_used, (NP + e + 1) * NB)
                if not first:
                    act.wait_ge(s_e2t, e)
                did("sT", nc.scalar.copy(colT, acc_blocks))
                act.wait_ge(s_e2t, e + 1)
                did("s_squares", nc.scalar.activation(squares, mm_blocks, ACT.Square))
                after_dve("relu")
                did("r_squares", nc.scalar.activation(spare, h_rows, ACT.Square))
                after_dve("floor_s")
                did("un", nc.scalar.activation(v["un"], v["s_sq"], ACT.Sqrt))
                act.wait_ge(s_e2a, step_value(E2_ACT, e, "un"))
                did("th", nc.scalar.activation(v["th"], v["un"], ACT.Tanh))
                after_dve("s_u")
                did("s_log", nc.scalar.activation(v["log"], v["u"], ACT.Ln))
                after_dve("floor_w")
                did("wn", nc.scalar.activation(v["wn"], v["w_sq"], ACT.Sqrt))
                act.wait_ge(s_e2a, step_value(E2_ACT, e, "wn"))
                did("tw", nc.scalar.activation(v["tw"], v["wn"], ACT.Tanh))
                after_dve("centered")
                did("centered_sq", nc.scalar.activation(squares, centered, ACT.Square))
                after_dve("variance")
                did("std", nc.scalar.activation(v["std"], v["variance"], ACT.Sqrt))

            epilogue1(0, first=True)
            with act.Fori(1, NP) as e:
                epilogue1(e)
            epilogue2(0, first=True)
            with act.Fori(1, NP) as e:
                epilogue2(e)

        @block.tensor
        def _(pe):
            pe.wait_ge(s_ident, 3)

            def panel(g, parity, n, early):
                i = g * NP + n
                if not early or n >= 2:
                    pe.wait_ge(s_added, i - 1)
                apart(pe)
                for u in range(GROUP):
                    for s in range(PARTS):
                        for h in range(PANEL // BANK):
                            col = n * PANEL + h * BANK
                            mm = nc.tensor.matmul(panel_ps[n % 2][:, h * BANK:(h + 1) * BANK],
                                                  x_parts[:, parity, s, u, :], adj8[:, parity, u, col:col + BANK],
                                                  start=(u == 0 and s == 0), stop=(u == GROUP - 1 and s == PARTS - 1))
                mm.then_inc(s_panel, 1)

            def turn(g, u, first):
                r = g * GROUP + u
                pe.wait_ge(s_packed16, r + 1)
                if not first:
                    pe.wait_ge(s_stored, r)
                for q in range(NQ):
                    mm = nc.tensor.transpose(packed_ps[:, q, :], packed16[:, q * P:(q + 1) * P], ident16[:, :])
                mm.then_inc(s_turned, 1)

            def sums(g, parity, u, first):
                r = g * GROUP + u
                pe.wait_ge(s_rs_ready, r + 1)
                apart(pe)
                for b in range(NB):
                    mm = nc.tensor.matmul(sums_ps[:, b, :], adj8[:, parity, u, b * P:(b + 1) * P],
                                          sum_parts[:, u % 2, 0:3], start=(first and b == 0), stop=True,
                                          skip_group_check=True)
                mm.then_inc(s_rs_used, 1)

            def group(g, parity, second=False):
                for u in range(GROUP):
                    if u == 0:
                        pe.wait_ge(s_conv, g * GROUP * NCH)
                        pe.wait_ge(s_xs, g)
                    panel(g - 1, 1 - parity, 2 * u, second)
                    panel(g - 1, 1 - parity, 2 * u + 1, second)
                    turn(g, u, False)
                    sums(g, parity, u, False)

            for u in range(GROUP):
                turn(0, u, u == 0)
                sums(0, 0, u, u == 0)
            group(1, 1, second=True)
            with pe.Fori(1, NG // 2) as pair:
                group(2 * pair, 0)
                group(2 * pair + 1, 1)
            pe.wait_ge(s_conv, NB * NCH)
            pe.wait_ge(s_xs, NG)
            for n in range(NP):
                panel(NG - 1, 1, n, False)

            def turn_y(b):
                pe.wait_ge(s_added, NG * NP)
                if b >= 2:
                    pe.wait_ge(s_ydve, 3 * (b - 2) + 1)
                for k in range(PB):
                    mm = nc.tensor.transpose(turn_ps[b % 2][:, k * P:(k + 1) * P],
                                             acc_space[:, (b * PB + k) * P:(b * PB + k + 1) * P], ident[:, :])
                mm.then_inc(s_yturn, 1)

            def contract(t, parts, q, first, fresh_parts=False):
                if fresh_parts:
                    pe.wait_ge(s_yact, 3 * (q + 1))
                for k in range(BITS):
                    pe.wait_ge(s_plane, t * NB + q * BITS + k + 1)
                    apart(pe)
                    for s in range(PARTS):
                        w = parts[:, s, q * BITS + k, :]
                        for h in range(PANEL // BANK):
                            mm = nc.tensor.matmul(acc[:, h * BANK:(h + 1) * BANK], w,
                                                  plane[:, k, h * BANK:(h + 1) * BANK].bitcast(F8),
                                                  start=(first and k == 0 and s == 0), stop=True,
                                                  skip_group_check=True)
                    mm.then_inc(s_used, 1)

            def add_x(t):
                pe.wait_ge(s_xsc, t + 1)
                for b in range(PB):
                    mm = nc.tensor.matmul(acc[:, b * P:(b + 1) * P], x_scaled[:, b, :], ident[:, :],
                                          start=False, stop=True, skip_group_check=True)
                mm.then_inc(s_acc, 1)

            def combine(e, first=False):
                if first:
                    pe.wait_ge(s_prep, 2)
                else:
                    pe.wait_ge(s_e1d, step_value(E1_DVE, e - 1, "h_part"))
                for b in range(PB):
                    mm = nc.tensor.matmul(mm_ps[:, b * P:(b + 1) * P], colT[:, b, :], V, start=True, stop=True)
                mm.then_inc(s_s1, 1)

            def turn_x1(e):
                pe.wait_ge(s_e1d, step_value(E1_DVE, e, "x1"))
                for b in range(PB):
                    mm = nc.tensor.transpose(tr_ps[:, b * P:(b + 1) * P], x1_rows[:, b, :], ident[:, :])
                mm.then_inc(s_s2, 1)

            def map_x1(e):
                pe.wait_ge(s_e1a, step_value(E1_ACT, e, "x1T"))
                for b in range(PB):
                    mm = nc.tensor.matmul(mm_ps[:, b * P:(b + 1) * P], colT[:, b, :], W1T, start=True, stop=True)
                mm.then_inc(s_s3, 1)

            def turn_s(e, first=False):
                if not first:
                    pe.wait_ge(s_e2d, step_value(E2_DVE, e - 1, "r_sq"))
                pe.wait_ge(s_e2a, step_value(E2_ACT, e, "sT"))
                for b in range(PB):
                    mm = nc.tensor.transpose(mm_ps[:, b * P:(b + 1) * P], colT[:, b, :], ident[:, :])
                mm.then_inc(s_e2t, 1)

            def contraction_with_epilogue1(t, parts, first=False):
                pe.wait_ge(s_e1a, step_value(E1_ACT, t - 1, "mT"))
                contract(t, parts, 0, True)
                combine(t - 1, first)
                for q in range(1, 3):
                    contract(t, parts, q, False)
                turn_x1(t - 1)
                contract(t, parts, 3, False)
                map_x1(t - 1)
                for q in range(4, NQ - 1):
                    contract(t, parts, q, False)

            turn_y(0)
            turn_y(1)
            for q in range(NQ):
                contract(0, y_parts, q, q == 0, fresh_parts=True)
                if q + 2 < NP:
                    turn_y(q + 2)
            pe.wait_ge(s_const, 48)
            nc.tensor.transpose(weights_ps[:, 0:C], w_in[:, 0, :], ident[:, :])
            nc.tensor.transpose(weights_ps[:, C:2 * C], w_in[:, 1, :], ident[:, :]).then_inc(s_wT, 1)
            add_x(0)

            def phase2_panel(t, first=False):
                contraction_with_epilogue1(t, y_parts, first)
                contract(t, y_parts, NQ - 1, False)
                add_x(t)

            phase2_panel(1, True)
            with pe.Fori(2, NP) as t:
                phase2_panel(t)
            contraction_with_epilogue1(NP, xt_parts)
            pe.wait_ge(s_e1a, step_value(E1_ACT, NP - 1, "part2"))
            contract(NP, xt_parts, NQ - 1, False)

            def contraction_with_epilogue2(t, first=False):
                pe.wait_ge(s_e2a, step_value(E2_ACT, t - NP - 1, "sT"))
                contract(t, xt_parts, 0, True)
                turn_s(t - NP - 1, first)
                for q in range(1, NQ):
                    contract(t, xt_parts, q, False)

            contraction_with_epilogue2(NP + 1, True)
            with pe.Fori(NP + 2, 2 * NP) as t:
                contraction_with_epilogue2(t)
            turn_s(NP - 1)

        @block.vector
        def _(dve):
            def chained(semaphore, value, ins):
                ins.then_inc(semaphore, 1)
                dve.wait_ge(semaphore, value)

            dve.wait_ge(s_ident, 4)

            def convert(g, parity, u, early):
                r = g * GROUP + u
                if not early and u == 0:
                    dve.wait_ge(s_panel, (g - 1) * NP)
                for c in range(NCH):
                    dve.wait_ge(s_adj[c], 16 * (r + 1))
                    apart(dve)
                    nc.vector.tensor_scalar(adj8[:, parity, u, c * CHUNK:(c + 1) * CHUNK], adj_in[:, c, :],
                                            1.0, TWO, ALU.is_equal, ALU.mult, saturate=False).then_inc(s_conv, 1)

            def pack(g, parity, u, first=False):
                r = g * GROUP + u
                dve.wait_ge(s_conv, NCH * (r + 1))
                if not first:
                    dve.wait_ge(s_packed16, r)
                src = adj8[:, parity, u, :].bitcast(U32).rearrange("p (q k w) -> p k q w", q=NQ, k=BITS)
                dst = packed.bitcast(U32).rearrange("p (q w) -> p q w", q=NQ)
                chained(s_pack, r * 7 + 1, nc.vector.tensor_scalar(dst, src[:, 0], 6, None, ALU.logical_shift_right))
                for k in range(1, BITS):
                    shift = ALU.logical_shift_right if k < 6 else ALU.logical_shift_left
                    ins = nc.vector.scalar_tensor_tensor(out=dst, in0=src[:, k], scalar=abs(6 - k), in1=dst,
                                                         op0=shift, op1=ALU.bitwise_or)
                    if k < BITS - 1:
                        chained(s_pack, r * 7 + k + 1, ins)
                    else:
                        ins.then_inc(s_packed, 1)

            def row_sum(g, u, first):
                r = g * GROUP + u
                dve.wait_ge(s_counted, NCH * (r + 1))
                d = degree[:, bass.ds(r, 1)]
                chained(s_summed, r + 1, nc.vector.tensor_reduce(d, row_counts[:, u % 2, :], AX, ALU.add))
                if not (first and u < 2):
                    dve.wait_ge(s_rs_used, r - 1)
                apart(dve)
                part = sum_parts[:, u % 2]
                chained(s_rs, r + 1, nc.vector.tensor_copy(part[:, 1:2], d))
                nc.vector.tensor_tensor(part[:, 2:3], d, part[:, 1:2], ALU.subtract).then_inc(s_rs_ready, 1)

            def add_panel(g, n, first=False):
                i = g * NP + n
                dve.wait_ge(s_panel, i + 1)
                dst = acc_space[:, n * PANEL:(n + 1) * PANEL]
                if first:
                    nc.vector.tensor_copy(dst, panel_ps[n % 2][:, :]).then_inc(s_added, 1)
                else:
                    nc.vector.tensor_tensor(dst, dst, panel_ps[n % 2][:, :], ALU.add).then_inc(s_added, 1)

            def group(g, parity, early=False):
                for u in range(GROUP):
                    convert(g, parity, u, early)
                    add_panel(g - 1, 2 * u, early)
                    pack(g, parity, u)
                    add_panel(g - 1, 2 * u + 1, early)
                    row_sum(g, u, False)

            for u in range(GROUP):
                convert(0, 0, u, True)
                pack(0, 0, u, first=(u == 0))
                row_sum(0, u, True)
            group(1, 1, early=True)
            with dve.Fori(1, NG // 2) as pair:
                group(2 * pair, 0)
                group(2 * pair + 1, 1)
            for n in range(NP):
                add_panel(NG - 1, n)

            dve.wait_ge(s_rs_used, NB)
            dve.wait_ge(s_added, NG * NP)
            nc.vector.tensor_copy(edge_ratio, sums_ps[:, :, 1]).then_inc(s_edge, 1)
            nc.vector.reciprocal(edge_root, sums_ps[:, :, 0]).then_inc(s_edge, 1)
            dve.wait_ge(s_edge, 2)
            chained(s_edge, 3, nc.vector.tensor_tensor(edge_ratio, edge_ratio, sums_ps[:, :, 2], ALU.add))
            chained(s_edge, 4, nc.vector.tensor_tensor(edge_ratio, edge_ratio, edge_root, ALU.mult))
            dve.wait_ge(s_edge_act, 2)
            chained(s_edge, 5, nc.vector.reciprocal(y_scale, edge_root))
            chained(s_edge, 6, nc.vector.tensor_scalar(y_scale, y_scale, 1.0 / (TWO * TWO), None, ALU.mult))
            chained(s_edge, 7, nc.vector.reciprocal(node_scale, degree_root))
            chained(s_edge, 8, nc.vector.tensor_scalar(node_scale, node_scale, 1.0 - ALPHA, None, ALU.mult))

            def split_y(b):
                sl = slice(b * PB, (b + 1) * PB)
                full = y_full[:, b % 2, :].rearrange("p (b c) -> p b c", b=PB)
                rest1 = y_rest[:, 2 * (b % 2), :].rearrange("p (b c) -> p b c", b=PB)
                rest2 = y_rest[:, 2 * (b % 2) + 1, :].rearrange("p (b c) -> p b c", b=PB)
                turned = turn_ps[b % 2][:, :].rearrange("p (b c) -> p b c", b=PB)
                dve.wait_ge(s_yturn, b + 1)
                if b >= 2:
                    dve.wait_ge(s_yact, 3 * (b - 1))
                chained(s_ydve, 3 * b + 1, nc.vector.tensor_tensor(full, turned, wide(y_scale[:, sl]), ALU.mult))
                dve.wait_ge(s_yact, 3 * b + 1)
                chained(s_ydve, 3 * b + 2, nc.vector.tensor_tensor(rest1, full, y_parts[:, 0, sl, :], ALU.subtract))
                dve.wait_ge(s_yact, 3 * b + 2)
                nc.vector.tensor_tensor(rest2, rest1, y_parts[:, 1, sl, :], ALU.subtract).then_inc(s_ydve, 1)

            def unpack(t, p, q, first=False):
                for k in range(BITS):
                    if not first:
                        dve.wait_ge(s_used, t * NB + q * BITS + k - BITS + 1)
                    shift = ALU.logical_shift_left if k <= 6 else ALU.logical_shift_right
                    src = adjT32[:, bass.ds(q, 1), bass.ds(p * (PANEL // 4), PANEL // 4)].rearrange("p o n -> p (o n)")
                    nc.vector.tensor_scalar(plane32[:, k, :], src, abs(6 - k), BIT, shift,
                                            ALU.bitwise_and).then_inc(s_plane, 1)

            def scale_x(t, first=False):
                dve.wait_ge(s_xrows, 16 * (t + 1))
                if not first:
                    dve.wait_ge(s_acc, t)
                nc.vector.scalar_tensor_tensor(out=x_scaled, in0=x_rows, scalar=ALPHA / (1.0 - ALPHA),
                                               in1=wide(degree_root[:, bass.ds(t * PB, PB)]),
                                               op0=ALU.mult, op1=ALU.mult).then_inc(s_xsc, 1)

            def steps(names, semaphore, e):
                order = iter(names)

                def did(name, ins):
                    assert next(order) == name, name
                    chained(semaphore, step_value(names, e, name), ins)
                return did

            def tt(out_, a, b, op):
                return nc.vector.tensor_tensor(out_, a, b, op)

            def ts(out_, a, s1, op1, s2=None, op2=ALU.bypass):
                return nc.vector.tensor_scalar(out_, a, s1, s2, op1, op2)

            def stt(out_, a, s, b, op0, op1):
                return nc.vector.scalar_tensor_tensor(out=out_, in0=a, scalar=s, in1=b, op0=op0, op1=op1)

            def log_argument(did, pre, v, c):
                did(pre + "one_minus", ts(v["om"], c, -1.0, ALU.mult, 1.0, ALU.add))
                did(pre + "inv_one_minus", nc.vector.reciprocal(v["iom"], v["om"]))
                did(pre + "v", stt(v["w"], c, 2.0, v["iom"], ALU.mult, ALU.mult))
                did(pre + "u", ts(v["u"], v["w"], 1.0, ALU.add))
                did(pre + "u_minus_1", ts(v["d"], v["u"], -1.0, ALU.add))
                did(pre + "is_one", ts(v["z"], v["d"], 0.0, ALU.is_equal))

            def log_result(did, pre, v):
                did(pre + "log_fixed", tt(v["lf"], v["log"], v["z"], ALU.add))
                did(pre + "denominator", tt(v["dd"], v["d"], v["z"], ALU.add))
                did(pre + "inv_denominator", nc.vector.reciprocal(v["idd"], v["dd"]))
                did(pre + "ratio", tt(v["rr"], v["w"], v["idd"], ALU.mult))
                did(pre + "atanh", stt(v["atanh"], v["lf"], 0.5, v["rr"], ALU.mult, ALU.mult))

            def normalize_1(did, v):
                did("row_sum", nc.vector.tensor_reduce(v["sum"], x1_rows, AX, ALU.add))
                did("mean", ts(v["mean"], v["sum"], 1.0 / C, ALU.mult))
                did("centered", tt(centered, x1_rows, wide(v["mean"]), ALU.subtract))

            def normalize_2(did, v, after_act, last):
                after_act("centered_sq")
                did("square_sum", nc.vector.tensor_reduce(v["sqs"], squares, AX, ALU.add))
                did("variance", ts(v["variance"], v["sqs"], 1.0 / C, ALU.mult, LN_EPS, ALU.add))
                after_act("std")
                did("inv_std", nc.vector.reciprocal(v["istd"], v["std"]))
                did(last, tt(x1_rows, centered, wide(v["istd"]), ALU.mult))

            def epilogue1(e, between, first=False):
                did = steps(E1_DVE, s_e1d, e)
                v = val1

                def after_act(name):
                    dve.wait_ge(s_e1a, step_value(E1_ACT, e, name))

                dve.wait_ge(s_s1, e + 1)
                if not first:
                    dve.wait_ge(s_x1out, 16 * e)
                did("scaled", tt(x1_rows, mm_blocks, wide(node_scale[:, bass.ds(e * PB, PB)]), ALU.mult))
                did("with_x", tt(x1_rows, x1_rows, x_rows, ALU.add))
                normalize_1(did, v)
                between(0)
                normalize_2(did, v, after_act, "x1")
                between(1)
                after_act("x1_squares")
                did("x_sq", nc.vector.tensor_reduce(v["x_sq"], squares, AX, ALU.add))
                after_act("mx_squares")
                did("mx_sq", nc.vector.tensor_reduce(v["mx_sq"], h_rows, AX, ALU.add))
                bias_wide = hyp_bias.unsqueeze(1).to_broadcast([P, PB, C])
                did("bias_product", tt(squares, mm_blocks, bias_wide, ALU.mult))
                did("dot", nc.vector.tensor_reduce(v["dot"], squares, AX, ALU.add))
                did("floor_x", ts(v["x_sq"], v["x_sq"], MIN_SQ, ALU.max))
                did("floor_mx", ts(v["mx_sq"], v["mx_sq"], MIN_SQ, ALU.max))
                after_act("mxn")
                did("clip_x", ts(v["c"], v["xn"], ATANH_CLIP, ALU.min))
                log_argument(did, "x_", v, v["c"])
                after_act("x_log")
                log_result(did, "x_", v)
                did("inv_xn", nc.vector.reciprocal(v["ixn"], v["xn"]))
                did("ratio_norms", tt(v["rn"], v["mxn"], v["ixn"], ALU.mult))
                did("tanh_arg", tt(v["tanh_arg"], v["rn"], v["atanh"], ALU.mult))
                after_act("tanh")
                did("t_clipped", ts(v["tc"], v["t"], MAX_NORM, ALU.min))
                did("inv_mxn", nc.vector.reciprocal(v["imxn"], v["mxn"]))
                did("a", tt(v["a"], v["tc"], v["imxn"], ALU.mult))
                did("aa", tt(v["aa"], v["a"], v["a"], ALU.mult))
                did("x2", tt(v["x2"], v["aa"], v["mx_sq"], ALU.mult))
                did("xy2", stt(v["xy2"], v["dot"], 2.0, v["a"], ALU.mult, ALU.mult))
                did("x2y2", ts(v["x2y2"], v["x2"], y2, ALU.mult))
                did("den", stt(v["den"], v["xy2"], 1.0, v["x2y2"], ALU.add, ALU.add))
                did("den_floor", ts(v["den"], v["den"], MIN_NORM, ALU.max))
                did("inv_den", nc.vector.reciprocal(v["iden"], v["den"]))
                did("num", ts(v["num"], v["xy2"], 1.0, ALU.add, y2, ALU.add))
                did("num_a", tt(v["na"], v["num"], v["a"], ALU.mult))
                did("A", tt(v["A"], v["na"], v["iden"], ALU.mult))
                did("one_minus_x2", ts(v["omx"], v["x2"], -1.0, ALU.mult, 1.0, ALU.add))
                did("B", tt(v["B"], v["omx"], v["iden"], ALU.mult))
                between(2)
                did("h_part", tt(h_rows, mm_blocks, wide(v["A"]), ALU.mult))
                did("b_part", tt(spare, bias_wide, wide(v["B"]), ALU.mult))
                did("h2", tt(h_rows, h_rows, spare, ALU.add))
                after_act("h_squares")
                did("h_sq", nc.vector.tensor_reduce(v["h_sq"], squares, AX, ALU.add))
                did("floor_h", ts(v["h_sq"], v["h_sq"], MIN_SQ, ALU.max))
                after_act("n2")
                did("clip_h", ts(v["c"], v["n2"], MAX_NORM, ALU.min))
                log_argument(did, "h_", v, v["c"])
                after_act("h_log")
                log_result(did, "h_", v)
                did("inv_n2", nc.vector.reciprocal(v["in2"], v["n2"]))
                did("kappa", stt(v["kappa"], v["atanh"], 1.0 / TWO, v["in2"], ALU.mult, ALU.mult))
                between(3)
                did("xt", tt(h_rows, h_rows, wide(v["kappa"]), ALU.mult))
                after_act("part0")
                blocks = bass.ds(e * PB, PB)
                did("rest1", tt(spare, h_rows, xt_parts[:, 0, blocks, :], ALU.subtract))
                after_act("part1")
                did("rest2", tt(squares, spare, xt_parts[:, 1, blocks, :], ALU.subtract))

            def epilogue2(e, between, first=False):
                did = steps(E2_DVE, s_e2d, e)
                v = val2

                def after_act(name):
                    dve.wait_ge(s_e2a, step_value(E2_ACT, e, name))

                dve.wait_ge(s_e2t, e + 1)
                after_act("s_squares")
                did("relu", ts(h_rows, mm_blocks, 0.0, ALU.max))
                did("s_sq", nc.vector.tensor_reduce(v["s_sq"], squares, AX, ALU.add))
                after_act("r_squares")
                did("r_sq", nc.vector.tensor_reduce(v["r_sq"], spare, AX, ALU.add))
                did("floor_s", ts(v["s_sq"], v["s_sq"], MIN_SQ, ALU.max))
                after_act("th")
                did("th_clipped", ts(v["c"], v["th"], MAX_NORM, ALU.min))
                log_argument(did, "s_", v, v["c"])
                after_act("s_log")
                log_result(did, "s_", v)
                did("inv_un", nc.vector.reciprocal(v["iun"], v["un"]))
                did("kappa", tt(v["kappa"], v["atanh"], v["iun"], ALU.mult))
                did("kk", tt(v["kk"], v["kappa"], v["kappa"], ALU.mult))
                did("w_sq", tt(v["w_sq"], v["kk"], v["r_sq"], ALU.mult))
                did("floor_w", ts(v["w_sq"], v["w_sq"], MIN_SQ, ALU.max))
                between(0)
                after_act("tw")
                did("tw_clipped", ts(v["twc"], v["tw"], MAX_NORM, ALU.min))
                did("inv_wn", nc.vector.reciprocal(v["iwn"], v["wn"]))
                did("kt", tt(v["kt"], v["kappa"], v["twc"], ALU.mult))
                did("kappa2", tt(v["k2"], v["kt"], v["iwn"], ALU.mult))
                dve.wait_ge(s_x1in, 16 * (e + 1))
                if not first:
                    dve.wait_ge(s_out, 16 * e)
                did("scaled", tt(x1_rows, h_rows, wide(v["k2"]), ALU.mult))
                did("with_x1", tt(x1_rows, x1_rows, x_rows, ALU.add))
                between(1)
                normalize_1(did, v)
                normalize_2(did, v, after_act, "out")

            def unpack_all(t, p, q0, q1):
                if q1 - q0 == 1:
                    unpack(t, p, q0)
                else:
                    apart(dve)
                    with dve.Fori(q0, q1) as q:
                        unpack(t, p, q)

            dve.wait_ge(s_stored, NB)
            for q in range(NQ):
                split_y(q)
                unpack(0, 0, q, first=(q == 0))
            bs = bias_stats
            scratch = squares[:, 0, :]
            dve.wait_ge(s_const, 48)
            chained(s_bias, 1, nc.vector.tensor_tensor(scratch, hyp_bias, hyp_bias, ALU.mult))
            chained(s_bias, 2, nc.vector.tensor_reduce(bs[:, 0:1], scratch, AX, ALU.add))
            chained(s_bias, 3, nc.vector.tensor_scalar(bs[:, 1:2], bs[:, 0:1], MIN_SQ, None, ALU.max))
            dve.wait_ge(s_bias_act, 2)
            chained(s_bias, 4, nc.vector.tensor_scalar(bs[:, 4:5], bs[:, 3:4], MAX_NORM, None, ALU.min))
            chained(s_bias, 5, nc.vector.reciprocal(bs[:, 5:6], bs[:, 2:3]))
            chained(s_bias, 6, nc.vector.tensor_tensor(bs[:, 6:7], bs[:, 4:5], bs[:, 5:6], ALU.mult))
            chained(s_bias, 7, nc.vector.tensor_scalar(hyp_bias, hyp_bias, bs[:, 6:7], None, ALU.mult))
            chained(s_bias, 8, nc.vector.tensor_tensor(scratch, hyp_bias, hyp_bias, ALU.mult))
            chained(s_bias, 9, nc.vector.tensor_reduce(bs[:, 7:8], scratch, AX, ALU.add))
            y2 = bs[:, 7:8]

            dve.wait_ge(s_wT, 1)
            assert BETA == 0.5
            chained(s_bias, 10, nc.vector.tensor_tensor(V, weights_ps[:, 0:C], ident[:, :], ALU.add))
            nc.vector.tensor_scalar(V, V, BETA, None, ALU.mult).then_inc(s_prep, 1)
            nc.vector.tensor_copy(W1T, weights_ps[:, C:2 * C]).then_inc(s_prep, 1)
            scale_x(0, first=True)

            def panel_with_epilogue1(t, p, first=False):
                def between(i):
                    unpack_all(t, p, *[(2, 3), (3, 5), (5, 6), (6, 7)][i])
                unpack_all(t, p, 0, 2)
                epilogue1(t - 1, between, first)
                unpack_all(t, p, 7, 8)

            panel_with_epilogue1(1, 1, first=True)
            scale_x(1)
            with dve.Fori(2, NP) as t:
                panel_with_epilogue1(t, t)
                scale_x(t)
            panel_with_epilogue1(NP, 0)

            def panel_with_epilogue2(t, first=False):
                def between(i):
                    unpack_all(t, t - NP, *[(2, 4), (4, 6)][i])
                unpack_all(t, t - NP, 0, 2)
                epilogue2(t - NP - 1, between, first)
                unpack_all(t, t - NP, 6, 8)

            panel_with_epilogue2(NP + 1, True)
            with dve.Fori(NP + 2, 2 * NP) as t:
                panel_with_epilogue2(t)
            epilogue2(NP - 1, lambda i: None)


_INS = ["x", "adj", "L0_gnn_W", "L1_gnn_weight", "L1_gnn_bias"]


def kernel(**inputs):
    import numpy as _np
    import concourse.bacc as _bacc
    from concourse import mybir as _mybir
    from concourse.bass_utils import run_bass_kernel_spmd as _run

    nc = _bacc.Bacc("TRN2", target_bir_lowering=False, num_devices=1)
    arrays, args = {}, []
    for name in _INS:
        a = _np.ascontiguousarray(inputs[name])
        arrays[f"in_{name}"] = a
        args.append(nc.dram_tensor(f"in_{name}", a.shape, _mybir.dt.from_np(a.dtype), kind="ExternalInput").ap())
    out = nc.dram_tensor("out_0", (N, C), _mybir.dt.float32, kind="ExternalOutput").ap()
    x1_dram = nc.dram_tensor("x1", (N, C), _mybir.dt.float32, kind="Internal").ap()
    build(nc, *args, out, x1_dram)
    r = _run(nc, [arrays], core_ids=[0])
    return r.results[0]["out_0"]
```

```python
from contextlib import ExitStack

import concourse.bass as bass
from concourse import mybir

P = 128
N = 8192
C = 128
NB = N // P
PARTS = 3
CHUNK = 2048
NCH = N // CHUNK
GROUP = 4
NG = NB // GROUP
PANEL = 1024
NP = N // PANEL
PB = PANEL // P
BANK = 512
BITS = 8
NQ = NB // BITS

ALPHA, BETA = 0.1, 0.5
LN_EPS = 1e-5
MIN_NORM = 1e-15
MIN_SQ = 1e-30
MAX_NORM = 1.0 - 1e-5
ATANH_CLIP = 1.0 - 1e-7
TWO = 2.0
BIT = 0x40404040

ALU = mybir.AluOpType
ACT = mybir.ActivationFunctionType
AX = mybir.AxisListType.X
F32 = mybir.dt.float32
BF16 = mybir.dt.bfloat16
F8 = mybir.dt.float8e4
U8 = mybir.dt.uint8
U32 = mybir.dt.uint32
I32 = mybir.dt.int32

ATANH = ["one_minus", "inv_one_minus", "v", "u", "u_minus_1", "is_one", "log_fixed", "denominator",
         "inv_denominator", "ratio", "atanh"]
E1_DVE = ["scaled", "with_x", "row_sum", "mean", "centered",
          "square_sum", "variance", "inv_std", "x1",
          "x_sq", "mx_sq", "bias_product", "dot", "floor_x", "floor_mx", "clip_x",
          *["x_" + s for s in ATANH],
          "inv_xn", "ratio_norms", "tanh_arg", "t_clipped", "inv_mxn", "a", "aa", "x2", "xy2",
          "x2y2", "den", "den_floor", "inv_den", "num", "num_a", "A", "one_minus_x2", "B",
          "h_part", "b_part", "h2", "h_sq", "floor_h", "clip_h",
          *["h_" + s for s in ATANH],
          "inv_n2", "kappa", "xt", "rest1", "rest2"]
E1_ACT = ["mT0", "mT1", "centered_sq", "std", "x1T", "x1_squares", "mx_squares", "xn", "mxn",
          "x_log", "tanh", "h_squares", "n2", "h_log", "part0", "part1", "part2"]
E2_DVE = ["relu", "s_sq", "r_sq", "floor_s", "th_clipped",
          *["s_" + s for s in ATANH],
          "inv_un", "kappa", "kk", "w_sq", "floor_w", "tw_clipped", "inv_wn", "kt", "kappa2",
          "scaled", "with_x1", "row_sum", "mean", "centered",
          "square_sum", "variance", "inv_std", "out"]
E2_ACT = ["sT0", "sT1", "s_squares", "r_squares", "un", "th", "s_log", "wn", "tw", "centered_sq", "std"]


def step_value(steps, round_, name):
    return round_ * len(steps) + steps.index(name) + 1


def build(nc, x, adj, W0, W1, bias, out, x1_dram):
    with ExitStack() as ctx:
        def sb(name, shape, dt):
            return ctx.enter_context(nc.sbuf_tensor(name, shape, dt))

        def sem(name):
            return ctx.enter_context(nc.semaphore(name))

        work = sb("work", [P, 96 * 1024], U8)
        adj_in = work[:, 0:32768].bitcast(F32).rearrange("p (s n) -> p s n", s=NCH)
        adj8 = work[:, 32768:98304].bitcast(F8).rearrange("p (g u n) -> p g u n", g=2, u=GROUP)
        split_bytes = PARTS * NB * C * 2
        y_parts = work[:, 0:split_bytes].bitcast(BF16).rearrange("p (s b c) -> p s b c", s=PARTS, b=NB)
        xt_parts = work[:, split_bytes:2 * split_bytes].bitcast(BF16).rearrange("p (s b c) -> p s b c", s=PARTS, b=NB)
        y_full = work[:, split_bytes:split_bytes + 8192].bitcast(F32).rearrange("p (s n) -> p s n", s=2)
        y_rest = work[:, split_bytes + 8192:split_bytes + 24576].bitcast(F32).rearrange("p (s n) -> p s n", s=4)
        adjT = sb("adjT", [P, NQ, N], U8)
        acc_space = sb("acc_space", [P, N], F32)
        rows = [acc_space[:, i * PANEL:(i + 1) * PANEL].rearrange("p (b c) -> p b c", b=PB) for i in range(8)]
        x_rows, x_scaled, colT, x1_rows, centered, squares, h_rows, spare = rows
        slots_space = sb("slots", [P, BITS * PANEL], U8)
        plane = slots_space[:, :].rearrange("p (k n) -> p k n", k=BITS)
        packed = slots_space[:, 0:1024]
        packed16 = slots_space[:, 1024:3072].bitcast(BF16)
        sink = slots_space[:, 3072:3072 + CHUNK]
        x_in = slots_space[:, 5120:7168].bitcast(F32).rearrange("p (u c) -> p u c", u=GROUP)
        small = sb("small", [P, 2 * GROUP * PARTS * C], BF16)
        x_parts = small[:, :].rearrange("p (g s u c) -> p g s u c", g=2, s=PARTS, u=GROUP)
        stats = small[:, :].bitcast(F32)
        ident = sb("ident", [P, P], F32)
        ident16 = sb("ident16", [P, P], BF16)
        degree = sb("degree", [P, NB], F32)
        row_counts = sb("row_counts", [P, 2, NCH], F32)
        sum_parts = sb("sum_parts", [P, 2, 4], BF16)
        bias_stats = sb("bias_stats", [P, 24], F32)
        flag = sb("flag", [P, 1], I32)

        ps = [ctx.enter_context(nc.psum_tensor(f"ps{i}", [P, PANEL], F32)) for i in range(4)]
        panel_ps = ps[0:2]
        sums_ps = ps[2][:, 0:3 * NB].rearrange("p (b v) -> p b v", b=NB)
        packed_ps = ps[2][:, BANK:2 * BANK].bitcast(BF16).rearrange("p (q i) -> p q i", q=NQ)
        weights_ps = ps[3]
        turn_ps = ps[0:2]
        acc = ps[2]
        mm_ps, tr_ps = ps[0], ps[1]

        s_adj = [sem(f"adj_loaded{i}") for i in range(NCH)]
        s_x = sem("x_loaded")
        s_const = sem("constants_loaded")
        s_ident = sem("identity_ready")
        s_wT = sem("weights_turned")
        s_prep = sem("weights_ready")
        s_bias = sem("bias_steps")
        s_bias_act = sem("bias_act")
        s_counted = sem("chunks_counted")
        s_conv = sem("chunks_converted")
        s_pack = sem("pack_steps")
        s_packed16 = sem("units_widened")
        s_turned = sem("units_turned")
        s_stored = sem("units_stored")
        s_summed = sem("rows_summed")
        s_rs = sem("row_sum_steps")
        s_rs_ready = sem("row_sums_ready")
        s_rs_used = sem("row_sums_used")
        s_xs_steps = sem("x_split_steps")
        s_xs = sem("x_split")
        s_apart = sem("waits_apart")
        s_flag_dve = sem("flag_steps")
        s_flag_pool = sem("flag_summed")
        s_flag = sem("flag_ready")
        s_gload = sem("general_chunk_loaded")
        s_gused = sem("general_chunk_used")
        s_gx = sem("general_x_loaded")
        s_gdve = sem("general_dve")
        s_gact = sem("general_act")
        s_gturned = sem("general_chunk_turned")
        s_gmm = sem("general_chunk_multiplied")
        s_grow = sem("general_rows_ready")
        s_gcol = sem("general_rows_turned")
        s_panel = sem("panels_multiplied")
        s_added = sem("panels_added")
        s_edge = sem("edge_steps")
        s_edge_act = sem("edge_act")
        s_yturn = sem("y_turned")
        s_ydve = sem("y_dve")
        s_yact = sem("y_act")
        s_plane = sem("planes_unpacked")
        s_used = sem("planes_used")
        s_acc = sem("panels_contracted")
        s_xrows = sem("x_rows_loaded")
        s_xsc = sem("x_scaled")
        s_e1d = sem("epilogue1_dve")
        s_e1a = sem("epilogue1_act")
        s_s1 = sem("epilogue1_combined")
        s_s2 = sem("epilogue1_turned")
        s_s3 = sem("epilogue1_mapped")
        s_x1out = sem("x1_stored")
        s_x1in = sem("x1_loaded")
        s_e2d = sem("epilogue2_dve")
        s_e2a = sem("epilogue2_act")
        s_e2t = sem("epilogue2_turned")
        s_out = sem("out_stored")

        adj_rows = adj.rearrange("(b p) n -> b p n", p=P)
        x_groups = x.rearrange("(g u p) c -> g p u c", u=GROUP, p=P)
        x_panels = x.rearrange("(t b p) c -> t p b c", b=PB, p=P)
        x1_panels = x1_dram.rearrange("(t b p) c -> t p b c", b=PB, p=P)
        out_panels = out.rearrange("(t b p) c -> t p b c", b=PB, p=P)

        def wide(v):
            return v.unsqueeze(2).to_broadcast([P, PB, C])

        gspace = adjT[:, :, :].rearrange("p q n -> p (q n)").bitcast(F32)
        XW = C + 2
        gx = gspace[:, 0:NB * XW].rearrange("p (b w) -> p b w", b=NB)
        gchunk = gspace[:, NB * XW:NB * XW + CHUNK]
        gturned = gspace[:, NB * XW + CHUNK:NB * XW + CHUNK + PANEL].rearrange("p (b c) -> p b c", b=PB)
        grow, gshare, gvals = [gspace[:, NB * XW + CHUNK + PANEL + i * C:][:, 0:C] for i in range(3)]
        gfull = work[:, 0:NB * C * 4].bitcast(F32).rearrange("p (b c) -> p b c", b=NB)
        G_SUMS = NB * NCH
        G_Y = G_SUMS + NB * PB
        G_XT = G_Y + NB * NP
        edge_ratio, edge_root, y_scale, degree_root, node_scale = [
            stats[:, i * NB:(i + 1) * NB] for i in range(5)]
        weights = stats[:, 5 * NB:5 * NB + 5 * C].rearrange("p (i c) -> p i c", i=5)
        w_in, V, W1T, hyp_bias = weights[:, 0:2], weights[:, 2], weights[:, 3], weights[:, 4]
        row_values = stats[:, 5 * NB + 5 * C:]

        class Row:

            def __init__(self, base):
                self.base, self.at = base, {}

            def __getitem__(self, name):
                i = self.base + self.at.setdefault(name, len(self.at))
                assert (i + 1) * PB <= row_values.shape[1]
                return row_values[:, i * PB:(i + 1) * PB]

        val1, val2 = Row(0), Row(0)
        mm_blocks = mm_ps[:, :].rearrange("p (b c) -> p b c", b=PB)
        tr_blocks = tr_ps[:, :].rearrange("p (b c) -> p b c", b=PB)
        acc_blocks = acc[:, :].rearrange("p (b c) -> p b c", b=PB)
        bank_blocks = [slice(h * BANK // P, (h + 1) * BANK // P) for h in range(2)]
        adjT32 = adjT[:, :, :].bitcast(U32)
        plane32 = plane[:, :, :].bitcast(U32)

        def apart(eng):
            eng.sem_inc(s_apart, 1)

        block = ctx.enter_context(nc.Block())

        @block.sync
        def _(sp):

            def load_row_block(r, first):
                for c in range(NCH):
                    if not first:
                        sp.wait_ge(s_counted, r * NCH + c - NCH + 1)
                        sp.wait_ge(s_conv, r * NCH + c - NCH + 1)
                    sp.dma_start(adj_in[:, c, :], adj_rows[r, :, c * CHUNK:(c + 1) * CHUNK]).then_inc(s_adj[c], 16)

            def load_x_group(g, first):
                if not first:
                    sp.wait_ge(s_xs, g)
                sp.dma_start(x_in[:, :, :], x_groups[g]).then_inc(s_x, 16)

            load_row_block(0, True)
            load_x_group(0, True)
            for u in range(1, GROUP):
                load_row_block(u, False)
            with sp.Fori(1, NG) as g:
                load_x_group(g, False)
                for u in range(GROUP):
                    load_row_block(g * GROUP + u, False)

            sp.wait_ge(s_flag, 1)
            not_binary = sp.value_load(flag[0:1, 0:1])
            sp.wait_ge(s_panel, NG * NP)
            sp.dma_start(w_in[:, 0, :], W0).then_inc(s_const, 16)
            sp.dma_start(w_in[:, 1, :], W1).then_inc(s_const, 16)
            sp.dma_start(hyp_bias, bias.unsqueeze(0).to_broadcast([P, C])).then_inc(s_const, 16)

            def x_panel(t, first):
                if not first:
                    sp.wait_ge(s_e1d, step_value(E1_DVE, t - 1, "with_x"))
                    sp.wait_ge(s_xsc, t)
                sp.dma_start(x_rows, x_panels[t]).then_inc(s_xrows, 16)

            def x1_store(e):
                sp.wait_ge(s_e1d, step_value(E1_DVE, e, "x1"))
                sp.dma_start(x1_panels[e], x1_rows).then_inc(s_x1out, 16)

            def x1_load(e, first):
                if not first:
                    sp.wait_ge(s_e2d, step_value(E2_DVE, e - 1, "with_x1"))
                sp.dma_start(x_rows, x1_panels[e]).then_inc(s_x1in, 16)

            def out_store(e):
                sp.wait_ge(s_e2d, step_value(E2_DVE, e, "out"))
                sp.dma_start(out_panels[e], x1_rows).then_inc(s_out, 16)

            def binary():
                sp.wait_ge(s_yturn, NP)
                x_panel(0, True)
                with sp.Fori(1, NP) as t:
                    x_panel(t, False)
                    x1_store(t - 1)
                x1_store(NP - 1)
                sp.wait_ge(s_x1out, 16 * NP)
                x1_load(0, True)
                with sp.Fori(1, NP) as e:
                    out_store(e - 1)
                    x1_load(e, False)
                out_store(NP - 1)
                sp.wait_ge(s_out, 16 * NP)

            def general():
                def chunk(n, dst, src):
                    sp.wait_ge(s_gused, n)
                    sp.dma_start(dst, src).then_inc(s_gload, 16)

                sp.wait_ge(s_stored, NB)
                sp.dma_start(gx[:, :, 0:C], x.rearrange("(b p) c -> p b c", p=P)).then_inc(s_gx, 16)
                sp.dma_start(gchunk, adj_rows[0, :, 0:CHUNK]).then_inc(s_gload, 16)
                for c in range(1, NCH):
                    chunk(c, gchunk, adj_rows[0, :, c * CHUNK:(c + 1) * CHUNK])
                with sp.Fori(1, NB) as r:
                    for c in range(NCH):
                        chunk(r * NCH + c, gchunk, adj_rows[r, :, c * CHUNK:(c + 1) * CHUNK])
                strips = adj.rearrange("(g k p) n -> g p k n", k=PB, p=P)
                with sp.Fori(0, NB) as j:
                    with sp.Fori(0, NB // PB) as g:
                        chunk(G_SUMS + j * PB + g, gchunk[:, 0:PANEL].rearrange("p (k n) -> p k n", k=PB),
                              strips[g][:, :, bass.ds(j * P, P)])

                def row_chunks(e, base):
                    with sp.Fori(0, PB) as b:
                        with sp.Fori(0, NP) as q:
                            chunk(base + e * NB + b * NP + q, gchunk[:, 0:PANEL],
                                  adj_rows[e * PB + b][:, bass.ds(q * PANEL, PANEL)])

                sp.wait_ge(s_added, NG * NP)
                x_panel(0, True)
                row_chunks(0, G_Y)
                x1_store(0)
                with sp.Fori(1, NP) as e:
                    x_panel(e, False)
                    row_chunks(e, G_Y)
                    x1_store(e)
                sp.wait_ge(s_x1out, 16 * NP)
                x1_load(0, True)
                row_chunks(0, G_XT)
                out_store(0)
                with sp.Fori(1, NP) as e:
                    x1_load(e, False)
                    row_chunks(e, G_XT)
                    out_store(e)
                sp.wait_ge(s_out, 16 * NP)

            with sp.If(not_binary == 0):
                binary()
            with sp.If(not_binary != 0):
                general()

        @block.gpsimd
        def _(pool):
            nc.gpsimd.memset(ident[:, :], 0.0).then_inc(s_ident, 1)
            pool.wait_ge(s_ident, 1)
            nc.gpsimd.affine_select(out=ident[:, :], in_=ident[:, :], compare_op=ALU.not_equal, fill=1.0,
                                    base=0, pattern=[[-1, P]], channel_multiplier=1).then_inc(s_ident, 1)
            pool.wait_ge(s_ident, 2)
            nc.gpsimd.tensor_copy(ident16[:, :], ident[:, :]).then_inc(s_ident, 1)
            nc.gpsimd.memset(sum_parts[:, :, :], 1.0).then_inc(s_ident, 1)

            def split_x(g, parity, early):
                pool.wait_ge(s_x, 16 * (g + 1))
                if not early:
                    pool.wait_ge(s_panel, (g - 1) * NP)
                apart(pool)
                part = x_parts[:, parity]
                nc.gpsimd.tensor_copy(part[:, 0], x_in[:, :, :]).then_inc(s_xs_steps, 1)
                pool.wait_ge(s_xs_steps, g * 4 + 1)
                apart(pool)
                nc.gpsimd.tensor_tensor(x_in[:, :, :], x_in[:, :, :], part[:, 0], ALU.subtract).then_inc(s_xs_steps, 1)
                pool.wait_ge(s_xs_steps, g * 4 + 2)
                apart(pool)
                nc.gpsimd.tensor_copy(part[:, 1], x_in[:, :, :]).then_inc(s_xs_steps, 1)
                pool.wait_ge(s_xs_steps, g * 4 + 3)
                apart(pool)
                nc.gpsimd.tensor_tensor(x_in[:, :, :], x_in[:, :, :], part[:, 1], ALU.subtract).then_inc(s_xs_steps, 1)
                pool.wait_ge(s_xs_steps, g * 4 + 4)
                apart(pool)
                nc.gpsimd.tensor_copy(part[:, 2], x_in[:, :, :]).then_inc(s_xs, 1)

            split_x(0, 0, early=True)
            split_x(1, 1, early=True)
            with pool.Fori(1, NG // 2) as pair:
                split_x(2 * pair, 0, early=False)
                split_x(2 * pair + 1, 1, early=False)

            pool.wait_ge(s_flag_dve, 7)
            nc.gpsimd.partition_all_reduce(bias_stats[:, 14:16], bias_stats[:, 12:14], P,
                                           bass.bass_isa.ReduceOp.add).then_inc(s_flag_pool, 1)

        @block.scalar
        def _(act):
            def count(r, parity):
                for c in range(NCH):
                    act.wait_ge(s_adj[c], 16 * (r + 1))
                    act.wait_ge(s_counted, r * NCH + c)
                    nc.scalar.activation(sink, adj_in[:, c, :].bitcast(U32), ACT.Sign,
                                         accum_out=row_counts[:, parity, c:c + 1]).then_inc(s_counted, 1)

            def store(r):
                act.wait_ge(s_turned, r + 1)
                nc.scalar.activation(adjT[:, :, bass.ds(r * P, P)], packed_ps, ACT.Copy).then_inc(s_stored, 1)

            count(0, 0)
            for u in range(1, GROUP):
                if u >= 2:
                    act.wait_ge(s_summed, u - 1)
                count(u, u % 2)
                store(u - 1)
            with act.Fori(1, NG) as g:
                for u in range(GROUP):
                    r = g * GROUP + u
                    act.wait_ge(s_summed, r - 1)
                    count(r, u % 2)
                    store(r - 1)
            store(NB - 1)

            act.wait_ge(s_flag, 1)
            not_binary = act.value_load(flag[0:1, 0:1])

            def roots_and_parts():
                act.wait_ge(s_edge, 4)
                nc.scalar.activation(edge_root, edge_ratio, ACT.Sqrt).then_inc(s_edge_act, 1)
                nc.scalar.activation(degree_root, degree[:, :], ACT.Sqrt).then_inc(s_edge_act, 1)
                for b in range(NP):
                    sl = slice(b * PB, (b + 1) * PB)
                    act.wait_ge(s_ydve, 3 * b + 1)
                    nc.scalar.activation(y_parts[:, 0, sl, :], y_full[:, b % 2, :].rearrange("p (b c) -> p b c", b=PB),
                                         ACT.Copy).then_inc(s_yact, 1)
                    act.wait_ge(s_ydve, 3 * b + 2)
                    nc.scalar.activation(y_parts[:, 1, sl, :], y_rest[:, 2 * (b % 2), :].rearrange("p (b c) -> p b c", b=PB),
                                         ACT.Copy).then_inc(s_yact, 1)
                    act.wait_ge(s_ydve, 3 * b + 3)
                    nc.scalar.activation(y_parts[:, 2, sl, :], y_rest[:, 2 * (b % 2) + 1, :].rearrange("p (b c) -> p b c", b=PB),
                                         ACT.Copy).then_inc(s_yact, 1)

            def bias_norm():
                act.wait_ge(s_bias, 3)
                nc.scalar.activation(bias_stats[:, 2:3], bias_stats[:, 1:2], ACT.Sqrt).then_inc(s_bias_act, 1)
                act.wait_ge(s_bias_act, 1)
                nc.scalar.activation(bias_stats[:, 3:4], bias_stats[:, 2:3], ACT.Tanh).then_inc(s_bias_act, 1)

            def epilogue1(r, contracted, first=False):
                def after_dve(name):
                    act.wait_ge(s_e1d, step_value(E1_DVE, r, name))

                order = iter(E1_ACT)

                def did(name, ins):
                    assert next(order) == name
                    ins.then_inc(s_e1a, 1)

                v = val1
                if not first:
                    act.wait_ge(s_s3, r)
                for h in range(2):
                    act.wait_ge(*contracted[h])
                    did(f"mT{h}", nc.scalar.copy(colT[:, bank_blocks[h]], acc_blocks[:, bank_blocks[h]]))
                after_dve("centered")
                did("centered_sq", nc.scalar.activation(squares, centered, ACT.Square))
                after_dve("variance")
                did("std", nc.scalar.activation(v["std"], v["variance"], ACT.Sqrt))
                act.wait_ge(s_s2, r + 1)
                did("x1T", nc.scalar.copy(colT, tr_blocks))
                did("x1_squares", nc.scalar.activation(squares, x1_rows, ACT.Square))
                act.wait_ge(s_s3, r + 1)
                did("mx_squares", nc.scalar.activation(h_rows, mm_blocks, ACT.Square))
                after_dve("floor_mx")
                did("xn", nc.scalar.activation(v["xn"], v["x_sq"], ACT.Sqrt))
                did("mxn", nc.scalar.activation(v["mxn"], v["mx_sq"], ACT.Sqrt))
                after_dve("x_u")
                did("x_log", nc.scalar.activation(v["log"], v["u"], ACT.Ln))
                after_dve("tanh_arg")
                did("tanh", nc.scalar.activation(v["t"], v["tanh_arg"], ACT.Tanh))
                after_dve("h2")
                did("h_squares", nc.scalar.activation(squares, h_rows, ACT.Square))
                after_dve("floor_h")
                did("n2", nc.scalar.activation(v["n2"], v["h_sq"], ACT.Sqrt))
                after_dve("h_u")
                did("h_log", nc.scalar.activation(v["log"], v["u"], ACT.Ln))
                for k, name in enumerate(["xt", "rest1", "rest2"]):
                    after_dve(name)
                    dst = xt_parts[:, k, bass.ds(r * PB, PB), :]
                    did(f"part{k}", nc.scalar.activation(dst, [h_rows, spare, squares][k], ACT.Copy))

            def epilogue2(r, contracted, first=False):
                def after_dve(name):
                    act.wait_ge(s_e2d, step_value(E2_DVE, r, name))

                order = iter(E2_ACT)

                def did(name, ins):
                    assert next(order) == name
                    ins.then_inc(s_e2a, 1)

                v = val2
                if not first:
                    act.wait_ge(s_e2t, r)
                for h in range(2):
                    act.wait_ge(*contracted[h])
                    did(f"sT{h}", nc.scalar.copy(colT[:, bank_blocks[h]], acc_blocks[:, bank_blocks[h]]))
                act.wait_ge(s_e2t, r + 1)
                did("s_squares", nc.scalar.activation(squares, mm_blocks, ACT.Square))
                after_dve("relu")
                did("r_squares", nc.scalar.activation(spare, h_rows, ACT.Square))
                after_dve("floor_s")
                did("un", nc.scalar.activation(v["un"], v["s_sq"], ACT.Sqrt))
                act.wait_ge(s_e2a, step_value(E2_ACT, r, "un"))
                did("th", nc.scalar.activation(v["th"], v["un"], ACT.Tanh))
                after_dve("s_u")
                did("s_log", nc.scalar.activation(v["log"], v["u"], ACT.Ln))
                after_dve("floor_w")
                did("wn", nc.scalar.activation(v["wn"], v["w_sq"], ACT.Sqrt))
                act.wait_ge(s_e2a, step_value(E2_ACT, r, "wn"))
                did("tw", nc.scalar.activation(v["tw"], v["wn"], ACT.Tanh))
                after_dve("centered")
                did("centered_sq", nc.scalar.activation(squares, centered, ACT.Square))
                after_dve("variance")
                did("std", nc.scalar.activation(v["std"], v["variance"], ACT.Sqrt))

            def binary():
                roots_and_parts()
                bias_norm()

                def banks(t):
                    return (s_acc, 2 * t + 1), (s_acc, 2 * t + 2)

                def banks_xt(e):
                    return (s_acc, 2 * NP + e + 1), (s_used, (NP + e + 1) * NB)

                epilogue1(0, banks(0), first=True)
                with act.Fori(1, NP) as e:
                    epilogue1(e, banks(e))
                epilogue2(0, banks_xt(0), first=True)
                with act.Fori(1, NP) as e:
                    epilogue2(e, banks_xt(e))

            def general():
                bias_norm()
                act.wait_ge(s_gdve, NB + 2)
                nc.scalar.activation(degree_root, degree[:, :], ACT.Sqrt).then_inc(s_gact, 1)
                with act.Fori(0, NB) as j:
                    act.wait_ge(s_gdve, NB + 4 + 4 * j + 2)
                    nc.scalar.activation(gvals[:, 2:3], gvals[:, 1:2], ACT.Sqrt).then_inc(s_gact, 1)

                def turned_chunk(n, base):
                    act.wait_ge(s_gused, base + n + 1)
                    nc.scalar.activation(gturned, tr_blocks, ACT.Copy, scale=TWO).then_inc(s_gturned, 1)


                def panel(e, base, epilogue, first=False):
                    with act.Fori(0, NB) as i:
                        turned_chunk(e * NB + i, base)
                    rows_before = 0 if base == G_Y else NB
                    turned = (s_gcol, rows_before + PB * (e + 1))
                    epilogue(e, (turned, turned), first)

                for base, epilogue in [(G_Y, epilogue1), (G_XT, epilogue2)]:
                    panel(0, base, epilogue, True)
                    with act.Fori(1, NP) as e:
                        panel(e, base, epilogue)

            with act.If(not_binary == 0):
                binary()
            with act.If(not_binary != 0):
                general()

        @block.tensor
        def _(pe):
            pe.wait_ge(s_ident, 3)

            def panel(g, parity, n, early):
                i = g * NP + n
                if not early or n >= 2:
                    pe.wait_ge(s_added, i - 1)
                apart(pe)
                for u in range(GROUP):
                    for s in range(PARTS):
                        for h in range(PANEL // BANK):
                            col = n * PANEL + h * BANK
                            mm = nc.tensor.matmul(panel_ps[n % 2][:, h * BANK:(h + 1) * BANK],
                                                  x_parts[:, parity, s, u, :], adj8[:, parity, u, col:col + BANK],
                                                  start=(u == 0 and s == 0), stop=(u == GROUP - 1 and s == PARTS - 1))
                mm.then_inc(s_panel, 1)

            def turn(g, u, first):
                r = g * GROUP + u
                pe.wait_ge(s_packed16, r + 1)
                if not first:
                    pe.wait_ge(s_stored, r)
                for q in range(NQ):
                    mm = nc.tensor.transpose(packed_ps[:, q, :], packed16[:, q * P:(q + 1) * P], ident16[:, :])
                mm.then_inc(s_turned, 1)

            def sums(g, parity, u, first):
                r = g * GROUP + u
                pe.wait_ge(s_rs_ready, r + 1)
                apart(pe)
                for b in range(NB):
                    mm = nc.tensor.matmul(sums_ps[:, b, :], adj8[:, parity, u, b * P:(b + 1) * P],
                                          sum_parts[:, u % 2, 0:3], start=(first and b == 0), stop=True,
                                          skip_group_check=True)
                mm.then_inc(s_rs_used, 1)

            def group(g, parity, second=False):
                for u in range(GROUP):
                    if u == 0:
                        pe.wait_ge(s_conv, g * GROUP * NCH)
                        pe.wait_ge(s_xs, g)
                    panel(g - 1, 1 - parity, 2 * u, second)
                    panel(g - 1, 1 - parity, 2 * u + 1, second)
                    turn(g, u, False)
                    sums(g, parity, u, False)

            for u in range(GROUP):
                turn(0, u, u == 0)
                sums(0, 0, u, u == 0)
            group(1, 1, second=True)
            with pe.Fori(1, NG // 2) as pair:
                group(2 * pair, 0)
                group(2 * pair + 1, 1)
            pe.wait_ge(s_conv, NB * NCH)
            pe.wait_ge(s_xs, NG)
            for n in range(NP):
                panel(NG - 1, 1, n, False)
                if n == NP // 2:
                    pe.wait_ge(s_flag, 1)
                    not_binary = pe.value_load(flag[0:1, 0:1])

            def turn_y(b):
                pe.wait_ge(s_added, NG * NP - (b == 0))
                if b >= 2:
                    pe.wait_ge(s_ydve, 3 * (b - 2) + 1)
                for k in range(PB):
                    mm = nc.tensor.transpose(turn_ps[b % 2][:, k * P:(k + 1) * P],
                                             acc_space[:, (b * PB + k) * P:(b * PB + k + 1) * P], ident[:, :])
                mm.then_inc(s_yturn, 1)

            def contract(t, parts, q, first, fresh_parts=False):
                if fresh_parts:
                    pe.wait_ge(s_yact, PARTS * (q + 1))
                for k in range(BITS):
                    pe.wait_ge(s_plane, t * NB + q * BITS + k + 1)
                    apart(pe)
                    for s in range(PARTS):
                        w = parts[:, s, q * BITS + k, :]
                        for h in range(PANEL // BANK):
                            mm = nc.tensor.matmul(acc[:, h * BANK:(h + 1) * BANK], w,
                                                  plane[:, k, h * BANK:(h + 1) * BANK].bitcast(F8),
                                                  start=(first and k == 0 and s == 0), stop=True,
                                                  skip_group_check=True)
                    mm.then_inc(s_used, 1)

            def contract_first():
                for s in range(PARTS):
                    pe.wait_ge(s_yact, s + 1)
                    for k in range(BITS):
                        if s == 0:
                            pe.wait_ge(s_plane, k + 1)
                        for h in range(PANEL // BANK):
                            mm = nc.tensor.matmul(acc[:, h * BANK:(h + 1) * BANK], y_parts[:, s, k, :],
                                                  plane[:, k, h * BANK:(h + 1) * BANK].bitcast(F8),
                                                  start=(k == 0 and s == 0), stop=True, skip_group_check=True)
                        if s == PARTS - 1:
                            mm.then_inc(s_used, 1)

            def contract_bank(t, parts, q, h, first):
                for k in range(BITS):
                    if h == 0:
                        pe.wait_ge(s_plane, t * NB + q * BITS + k + 1)
                        apart(pe)
                    for s in range(PARTS):
                        mm = nc.tensor.matmul(acc[:, h * BANK:(h + 1) * BANK], parts[:, s, q * BITS + k, :],
                                              plane[:, k, h * BANK:(h + 1) * BANK].bitcast(F8),
                                              start=(first and k == 0 and s == 0), stop=True,
                                              skip_group_check=True)
                    if h == 1:
                        mm.then_inc(s_used, 1)
                return mm

            def contract_start(t, parts, copied):
                for h in range(2):
                    copied(h)
                    contract_bank(t, parts, 0, h, True)

            def contract_end_with_x(t, parts):
                for h in range(2):
                    contract_bank(t, parts, NQ - 1, h, False)
                    pe.wait_ge(s_xsc, t + 1)
                    for b in range(*bank_blocks[h].indices(PB)):
                        mm = nc.tensor.matmul(acc[:, b * P:(b + 1) * P], x_scaled[:, b, :], ident[:, :],
                                              start=False, stop=True, skip_group_check=True)
                    mm.then_inc(s_acc, 1)

            def contract_end(t, parts):
                contract_bank(t, parts, NQ - 1, 0, False).then_inc(s_acc, 1)
                contract_bank(t, parts, NQ - 1, 1, False)

            def combine(r, first=False):
                if first:
                    pe.wait_ge(s_prep, 2)
                else:
                    pe.wait_ge(s_e1d, step_value(E1_DVE, r - 1, "h_part"))
                pe.wait_ge(s_e1a, step_value(E1_ACT, r, "mT1"))
                for b in range(PB):
                    mm = nc.tensor.matmul(mm_ps[:, b * P:(b + 1) * P], colT[:, b, :], V, start=True, stop=True)
                mm.then_inc(s_s1, 1)

            def turn_x1(r):
                pe.wait_ge(s_e1d, step_value(E1_DVE, r, "x1"))
                for b in range(PB):
                    mm = nc.tensor.transpose(tr_ps[:, b * P:(b + 1) * P], x1_rows[:, b, :], ident[:, :])
                mm.then_inc(s_s2, 1)

            def map_x1(r):
                pe.wait_ge(s_e1a, step_value(E1_ACT, r, "x1T"))
                for b in range(PB):
                    mm = nc.tensor.matmul(mm_ps[:, b * P:(b + 1) * P], colT[:, b, :], W1T, start=True, stop=True)
                mm.then_inc(s_s3, 1)

            def turn_s(r, first=False):
                if not first:
                    pe.wait_ge(s_e2d, step_value(E2_DVE, r - 1, "r_sq"))
                pe.wait_ge(s_e2a, step_value(E2_ACT, r, "sT1"))
                for b in range(PB):
                    mm = nc.tensor.transpose(mm_ps[:, b * P:(b + 1) * P], colT[:, b, :], ident[:, :])
                mm.then_inc(s_e2t, 1)

            def contraction_with_epilogue1(t, parts, first=False):
                def copied(h):
                    pe.wait_ge(s_e1a, step_value(E1_ACT, t - 1, f"mT{h}"))
                    apart(pe)

                contract_start(t, parts, copied)
                combine(t - 1, first)
                for q in range(1, 3):
                    contract(t, parts, q, False)
                turn_x1(t - 1)
                contract(t, parts, 3, False)
                map_x1(t - 1)
                for q in range(4, NQ - 1):
                    contract(t, parts, q, False)

            def turn_weights():
                pe.wait_ge(s_const, 48)
                nc.tensor.transpose(weights_ps[:, 0:C], w_in[:, 0, :], ident[:, :])
                nc.tensor.transpose(weights_ps[:, C:2 * C], w_in[:, 1, :], ident[:, :]).then_inc(s_wT, 1)

            def phase2_panel(t, first=False):
                contraction_with_epilogue1(t, y_parts, first)
                contract_end_with_x(t, y_parts)

            def contraction_with_epilogue2(t, first=False):
                def copied(h):
                    pe.wait_ge(s_e2a, step_value(E2_ACT, t - NP - 1, f"sT{h}"))
                    apart(pe)

                contract_start(t, xt_parts, copied)
                turn_s(t - NP - 1, first)
                for q in range(1, NQ - 1):
                    contract(t, xt_parts, q, False)
                contract_end(t, xt_parts)

            def binary():
                turn_y(0)
                turn_y(1)
                contract_first()
                turn_y(2)
                for q in range(1, NQ - 1):
                    contract(0, y_parts, q, False, fresh_parts=True)
                    if q + 2 < NP:
                        turn_y(q + 2)
                turn_weights()
                pe.wait_ge(s_yact, PARTS * NQ)
                contract_end_with_x(0, y_parts)
                phase2_panel(1, True)
                with pe.Fori(2, NP) as t:
                    phase2_panel(t)
                contraction_with_epilogue1(NP, xt_parts)
                pe.wait_ge(s_e1a, step_value(E1_ACT, NP - 1, "part2"))
                contract_end(NP, xt_parts)
                contraction_with_epilogue2(NP + 1, True)
                with pe.Fori(NP + 2, 2 * NP) as t:
                    contraction_with_epilogue2(t)
                turn_s(NP - 1)

            def general():
                turn_weights()
                pe.wait_ge(s_prep, 2)
                pe.wait_ge(s_gx, 16)
                pe.wait_ge(s_gdve, NB + 2)
                sums = weights_ps[:, 0:XW]

                def strip(j, g, first):
                    pe.wait_ge(s_gload, 16 * (G_SUMS + 1) + 16 * (j * PB + g))
                    for k in range(PB):
                        mm = nc.tensor.matmul(sums, gchunk[:, k * P:(k + 1) * P],
                                              gx[:, bass.ds(g * PB + k, 1), :].rearrange("p o w -> p (o w)"),
                                              start=(first and k == 0), stop=True, skip_group_check=True)
                    mm.then_inc(s_gused, 1)

                with pe.Fori(0, NB) as j:
                    pe.wait_ge(s_gdve, NB + 4 + 4 * j)
                    strip(j, 0, True)
                    with pe.Fori(1, NB // PB) as g:
                        strip(j, g, False)

                def row_chunk(n, q, base, first):
                    pe.wait_ge(s_gload, 16 * (base + 1) + 16 * n)
                    for k in range(PB):
                        mm = nc.tensor.transpose(tr_ps[:, k * P:(k + 1) * P], gchunk[:, k * P:(k + 1) * P], ident[:, :])
                    mm.then_inc(s_gused, 1)
                    pe.wait_ge(s_gturned, (base - G_Y + 1) + n)
                    for k in range(PB):
                        mm = nc.tensor.matmul(weights_ps[:, 0:C], gturned[:, k, :],
                                              gfull[:, bass.ds(q * PB + k, 1), :].rearrange("p o c -> p (o c)"),
                                              start=(first and k == 0), stop=True, skip_group_check=True)
                    mm.then_inc(s_gmm, 1)

                def panel_rows(e, base):
                    with pe.Fori(0, PB) as b:
                        n = e * NB + b * NP
                        row_chunk(n, 0, base, True)
                        with pe.Fori(1, NP) as q:
                            row_chunk(n + q, q, base, False)
                        pe.wait_ge(s_grow, ((base - G_Y) // NP + 1) + e * PB + b)
                        nc.tensor.matmul(acc[:, bass.ds(b * P, P)], grow, ident[:, :],
                                         start=True, stop=True, skip_group_check=True).then_inc(s_gcol, 1)

                pe.wait_ge(s_gdve, NB + 4 + 4 * NB)

                def panel_y(e, first=False):
                    panel_rows(e, G_Y)
                    combine(e, first)
                    turn_x1(e)
                    map_x1(e)

                def panel_xt(e, first=False):
                    panel_rows(e, G_XT)
                    turn_s(e, first)

                panel_y(0, True)
                with pe.Fori(1, NP) as e:
                    panel_y(e)
                pe.wait_ge(s_gdve, NB + 4 + 4 * NB + 2 * NP)
                panel_xt(0, True)
                with pe.Fori(1, NP) as e:
                    panel_xt(e)

            with pe.If(not_binary == 0):
                binary()
            with pe.If(not_binary != 0):
                general()

        @block.vector
        def _(dve):
            def chained(semaphore, value, ins):
                ins.then_inc(semaphore, 1)
                dve.wait_ge(semaphore, value)

            dve.wait_ge(s_ident, 4)

            def convert(g, parity, u, early):
                r = g * GROUP + u
                if not early and u == 0:
                    dve.wait_ge(s_panel, (g - 1) * NP)
                for c in range(NCH):
                    dve.wait_ge(s_adj[c], 16 * (r + 1))
                    apart(dve)
                    nc.vector.tensor_scalar(adj8[:, parity, u, c * CHUNK:(c + 1) * CHUNK], adj_in[:, c, :],
                                            1.0, TWO, ALU.is_equal, ALU.mult, saturate=False).then_inc(s_conv, 1)

            def pack(g, parity, u, first=False):
                r = g * GROUP + u
                dve.wait_ge(s_conv, NCH * (r + 1))
                src = adj8[:, parity, u, :].bitcast(U32).rearrange("p (q k w) -> p k q w", q=NQ, k=BITS)
                dst = packed.bitcast(U32).rearrange("p (q w) -> p q w", q=NQ)
                chained(s_pack, r * BITS + 1, nc.vector.tensor_scalar(dst, src[:, 0], 6, None, ALU.logical_shift_right))
                for k in range(1, BITS):
                    shift = ALU.logical_shift_right if k < 6 else ALU.logical_shift_left
                    ins = nc.vector.scalar_tensor_tensor(out=dst, in0=src[:, k], scalar=abs(6 - k), in1=dst,
                                                         op0=shift, op1=ALU.bitwise_or)
                    chained(s_pack, r * BITS + k + 1, ins)
                if not first:
                    dve.wait_ge(s_turned, r)
                    apart(dve)
                nc.vector.tensor_copy(packed16, packed).then_inc(s_packed16, 1)

            def row_sum(g, u, first):
                r = g * GROUP + u
                dve.wait_ge(s_counted, NCH * (r + 1))
                d = degree[:, bass.ds(r, 1)]
                chained(s_summed, r + 1, nc.vector.tensor_reduce(d, row_counts[:, u % 2, :], AX, ALU.add))
                if not (first and u < 2):
                    dve.wait_ge(s_rs_used, r - 1)
                apart(dve)
                part = sum_parts[:, u % 2]
                chained(s_rs, r + 1, nc.vector.tensor_copy(part[:, 1:2], d))
                nc.vector.tensor_tensor(part[:, 2:3], d, part[:, 1:2], ALU.subtract).then_inc(s_rs_ready, 1)

            def add_panel(g, n, first=False):
                i = g * NP + n
                dve.wait_ge(s_panel, i + 1)
                dst = acc_space[:, n * PANEL:(n + 1) * PANEL]
                if first:
                    nc.vector.tensor_copy(dst, panel_ps[n % 2][:, :]).then_inc(s_added, 1)
                else:
                    nc.vector.tensor_tensor(dst, dst, panel_ps[n % 2][:, :], ALU.add).then_inc(s_added, 1)

            def group(g, parity, early=False):
                for u in range(GROUP):
                    convert(g, parity, u, early)
                    pack(g, parity, u)
                    add_panel(g - 1, 2 * u, early)
                    row_sum(g, u, False)
                    add_panel(g - 1, 2 * u + 1, early)

            for u in range(GROUP):
                convert(0, 0, u, True)
                pack(0, 0, u, first=(u == 0))
                row_sum(0, u, True)
            group(1, 1, early=True)
            with dve.Fori(1, NG // 2) as pair:
                group(2 * pair, 0)
                group(2 * pair + 1, 1)
            add_panel(NG - 1, 0)
            fl = bias_stats
            dve.wait_ge(s_rs_used, NB)
            nc.vector.tensor_reduce(fl[:, 8:9], sums_ps[:, :, 0], AX, ALU.add).then_inc(s_flag_dve, 1)
            nc.vector.tensor_reduce(fl[:, 9:10], degree[:, :], AX, ALU.add).then_inc(s_flag_dve, 1)
            dve.wait_ge(s_flag_dve, 2)
            chained(s_flag_dve, 3, nc.vector.scalar_tensor_tensor(
                out=fl[:, 10:11].bitcast(I32), in0=fl[:, 9:10], scalar=-TWO, in1=fl[:, 8:9], op0=ALU.mult, op1=ALU.add))
            nc.vector.tensor_scalar(fl[:, 16:17].bitcast(I32), fl[:, 10:11].bitcast(I32), 1023, None,
                                    ALU.bitwise_and).then_inc(s_flag_dve, 1)
            nc.vector.tensor_scalar(fl[:, 17:18].bitcast(I32), fl[:, 10:11].bitcast(I32), 10, None,
                                    ALU.arith_shift_right).then_inc(s_flag_dve, 1)
            dve.wait_ge(s_flag_dve, 5)
            nc.vector.tensor_copy(fl[:, 12:13], fl[:, 16:17].bitcast(I32)).then_inc(s_flag_dve, 1)
            nc.vector.tensor_copy(fl[:, 13:14], fl[:, 17:18].bitcast(I32)).then_inc(s_flag_dve, 1)

            add_panel(NG - 1, 1)
            add_panel(NG - 1, 2)
            dve.wait_ge(s_flag_pool, 1)
            chained(s_flag_dve, 8, nc.vector.scalar_tensor_tensor(
                out=fl[:, 18:19], in0=fl[:, 15:16], scalar=1024.0, in1=fl[:, 14:15], op0=ALU.mult, op1=ALU.add))
            nc.vector.tensor_scalar(flag[:, :], fl[:, 18:19], 0.0, None, ALU.not_equal).then_inc(s_flag, 1)
            add_panel(NG - 1, 3)
            dve.wait_ge(s_flag, 1)
            not_binary = dve.value_load(flag[0:1, 0:1])

            def edge_degrees():
                dve.wait_ge(s_panel, (NG - 1) * NP)
                nc.vector.tensor_copy(edge_ratio, sums_ps[:, :, 1]).then_inc(s_edge, 1)
                nc.vector.reciprocal(edge_root, sums_ps[:, :, 0]).then_inc(s_edge, 1)
                dve.wait_ge(s_edge, 2)
                chained(s_edge, 3, nc.vector.tensor_tensor(edge_ratio, edge_ratio, sums_ps[:, :, 2], ALU.add))
                chained(s_edge, 4, nc.vector.tensor_tensor(edge_ratio, edge_ratio, edge_root, ALU.mult))
                dve.wait_ge(s_edge_act, 2)
                chained(s_edge, 5, nc.vector.reciprocal(y_scale, edge_root))
                chained(s_edge, 6, nc.vector.tensor_scalar(y_scale, y_scale, 1.0 / (TWO * TWO), None, ALU.mult))
                chained(s_edge, 7, nc.vector.reciprocal(node_scale, degree_root))
                chained(s_edge, 8, nc.vector.tensor_scalar(node_scale, node_scale, 1.0 - ALPHA, None, ALU.mult))

            def split_y(b):
                sl = slice(b * PB, (b + 1) * PB)
                full = y_full[:, b % 2, :].rearrange("p (b c) -> p b c", b=PB)
                rest1 = y_rest[:, 2 * (b % 2), :].rearrange("p (b c) -> p b c", b=PB)
                rest2 = y_rest[:, 2 * (b % 2) + 1, :].rearrange("p (b c) -> p b c", b=PB)
                turned = turn_ps[b % 2][:, :].rearrange("p (b c) -> p b c", b=PB)
                dve.wait_ge(s_yturn, b + 1)
                if b >= 2:
                    dve.wait_ge(s_yact, 3 * (b - 1))
                chained(s_ydve, 3 * b + 1, nc.vector.tensor_tensor(full, turned, wide(y_scale[:, sl]), ALU.mult))
                dve.wait_ge(s_yact, 3 * b + 1)
                chained(s_ydve, 3 * b + 2, nc.vector.tensor_tensor(rest1, full, y_parts[:, 0, sl, :], ALU.subtract))
                dve.wait_ge(s_yact, 3 * b + 2)
                nc.vector.tensor_tensor(rest2, rest1, y_parts[:, 1, sl, :], ALU.subtract).then_inc(s_ydve, 1)

            def unpack(t, p, q, first=False):
                for k in range(BITS):
                    if not first:
                        dve.wait_ge(s_used, t * NB + q * BITS + k - BITS + 1)
                    shift = ALU.logical_shift_left if k <= 6 else ALU.logical_shift_right
                    src = adjT32[:, bass.ds(q, 1), bass.ds(p * (PANEL // 4), PANEL // 4)].rearrange("p o n -> p (o n)")
                    nc.vector.tensor_scalar(plane32[:, k, :], src, abs(6 - k), BIT, shift,
                                            ALU.bitwise_and).then_inc(s_plane, 1)

            def scale_x(t, first=False):
                dve.wait_ge(s_xrows, 16 * (t + 1))
                if not first:
                    dve.wait_ge(s_acc, 2 * t)
                nc.vector.scalar_tensor_tensor(out=x_scaled, in0=x_rows, scalar=ALPHA / (1.0 - ALPHA),
                                               in1=wide(degree_root[:, bass.ds(t * PB, PB)]),
                                               op0=ALU.mult, op1=ALU.mult).then_inc(s_xsc, 1)

            def steps(names, semaphore, r):
                order = iter(names)

                def did(name, ins):
                    assert next(order) == name, name
                    chained(semaphore, step_value(names, r, name), ins)
                return did

            def tt(out_, a, b, op):
                return nc.vector.tensor_tensor(out_, a, b, op)

            def ts(out_, a, s1, op1, s2=None, op2=ALU.bypass):
                return nc.vector.tensor_scalar(out_, a, s1, s2, op1, op2)

            def stt(out_, a, s, b, op0, op1):
                return nc.vector.scalar_tensor_tensor(out=out_, in0=a, scalar=s, in1=b, op0=op0, op1=op1)

            def log_argument(did, pre, v, c):
                did(pre + "one_minus", ts(v["om"], c, -1.0, ALU.mult, 1.0, ALU.add))
                did(pre + "inv_one_minus", nc.vector.reciprocal(v["iom"], v["om"]))
                did(pre + "v", stt(v["w"], c, 2.0, v["iom"], ALU.mult, ALU.mult))
                did(pre + "u", ts(v["u"], v["w"], 1.0, ALU.add))
                did(pre + "u_minus_1", ts(v["d"], v["u"], -1.0, ALU.add))
                did(pre + "is_one", ts(v["z"], v["d"], 0.0, ALU.is_equal))

            def log_result(did, pre, v):
                did(pre + "log_fixed", tt(v["lf"], v["log"], v["z"], ALU.add))
                did(pre + "denominator", tt(v["dd"], v["d"], v["z"], ALU.add))
                did(pre + "inv_denominator", nc.vector.reciprocal(v["idd"], v["dd"]))
                did(pre + "ratio", tt(v["rr"], v["w"], v["idd"], ALU.mult))
                did(pre + "atanh", stt(v["atanh"], v["lf"], 0.5, v["rr"], ALU.mult, ALU.mult))

            def normalize_1(did, v):
                did("row_sum", nc.vector.tensor_reduce(v["sum"], x1_rows, AX, ALU.add))
                did("mean", ts(v["mean"], v["sum"], 1.0 / C, ALU.mult))
                did("centered", tt(centered, x1_rows, wide(v["mean"]), ALU.subtract))

            def normalize_2(did, v, after_act, last):
                after_act("centered_sq")
                did("square_sum", nc.vector.tensor_reduce(v["sqs"], squares, AX, ALU.add))
                did("variance", ts(v["variance"], v["sqs"], 1.0 / C, ALU.mult, LN_EPS, ALU.add))
                after_act("std")
                did("inv_std", nc.vector.reciprocal(v["istd"], v["std"]))
                did(last, tt(x1_rows, centered, wide(v["istd"]), ALU.mult))

            def epilogue1(r, between, first=False):
                did = steps(E1_DVE, s_e1d, r)
                v = val1

                def after_act(name):
                    dve.wait_ge(s_e1a, step_value(E1_ACT, r, name))

                dve.wait_ge(s_s1, r + 1)
                if not first:
                    dve.wait_ge(s_x1out, 16 * r)
                did("scaled", tt(x1_rows, mm_blocks, wide(node_scale[:, bass.ds(r * PB, PB)]), ALU.mult))
                did("with_x", tt(x1_rows, x1_rows, x_rows, ALU.add))
                normalize_1(did, v)
                between(0)
                normalize_2(did, v, after_act, "x1")
                between(1)
                after_act("x1_squares")
                did("x_sq", nc.vector.tensor_reduce(v["x_sq"], squares, AX, ALU.add))
                after_act("mx_squares")
                did("mx_sq", nc.vector.tensor_reduce(v["mx_sq"], h_rows, AX, ALU.add))
                bias_wide = hyp_bias.unsqueeze(1).to_broadcast([P, PB, C])
                did("bias_product", tt(squares, mm_blocks, bias_wide, ALU.mult))
                did("dot", nc.vector.tensor_reduce(v["dot"], squares, AX, ALU.add))
                did("floor_x", ts(v["x_sq"], v["x_sq"], MIN_SQ, ALU.max))
                did("floor_mx", ts(v["mx_sq"], v["mx_sq"], MIN_SQ, ALU.max))
                after_act("mxn")
                did("clip_x", ts(v["c"], v["xn"], ATANH_CLIP, ALU.min))
                log_argument(did, "x_", v, v["c"])
                after_act("x_log")
                log_result(did, "x_", v)
                between(2)
                did("inv_xn", nc.vector.reciprocal(v["ixn"], v["xn"]))
                did("ratio_norms", tt(v["rn"], v["mxn"], v["ixn"], ALU.mult))
                did("tanh_arg", tt(v["tanh_arg"], v["rn"], v["atanh"], ALU.mult))
                after_act("tanh")
                did("t_clipped", ts(v["tc"], v["t"], MAX_NORM, ALU.min))
                did("inv_mxn", nc.vector.reciprocal(v["imxn"], v["mxn"]))
                did("a", tt(v["a"], v["tc"], v["imxn"], ALU.mult))
                did("aa", tt(v["aa"], v["a"], v["a"], ALU.mult))
                did("x2", tt(v["x2"], v["aa"], v["mx_sq"], ALU.mult))
                did("xy2", stt(v["xy2"], v["dot"], 2.0, v["a"], ALU.mult, ALU.mult))
                did("x2y2", ts(v["x2y2"], v["x2"], y2, ALU.mult))
                did("den", stt(v["den"], v["xy2"], 1.0, v["x2y2"], ALU.add, ALU.add))
                did("den_floor", ts(v["den"], v["den"], MIN_NORM, ALU.max))
                did("inv_den", nc.vector.reciprocal(v["iden"], v["den"]))
                did("num", ts(v["num"], v["xy2"], 1.0, ALU.add, y2, ALU.add))
                did("num_a", tt(v["na"], v["num"], v["a"], ALU.mult))
                did("A", tt(v["A"], v["na"], v["iden"], ALU.mult))
                did("one_minus_x2", ts(v["omx"], v["x2"], -1.0, ALU.mult, 1.0, ALU.add))
                did("B", tt(v["B"], v["omx"], v["iden"], ALU.mult))
                did("h_part", tt(h_rows, mm_blocks, wide(v["A"]), ALU.mult))
                did("b_part", tt(spare, bias_wide, wide(v["B"]), ALU.mult))
                did("h2", tt(h_rows, h_rows, spare, ALU.add))
                between(3)
                after_act("h_squares")
                did("h_sq", nc.vector.tensor_reduce(v["h_sq"], squares, AX, ALU.add))
                did("floor_h", ts(v["h_sq"], v["h_sq"], MIN_SQ, ALU.max))
                after_act("n2")
                did("clip_h", ts(v["c"], v["n2"], MAX_NORM, ALU.min))
                log_argument(did, "h_", v, v["c"])
                after_act("h_log")
                log_result(did, "h_", v)
                did("inv_n2", nc.vector.reciprocal(v["in2"], v["n2"]))
                did("kappa", stt(v["kappa"], v["atanh"], 1.0 / TWO, v["in2"], ALU.mult, ALU.mult))
                did("xt", tt(h_rows, h_rows, wide(v["kappa"]), ALU.mult))
                between(4)
                after_act("part0")
                blocks = bass.ds(r * PB, PB)
                did("rest1", tt(spare, h_rows, xt_parts[:, 0, blocks, :], ALU.subtract))
                after_act("part1")
                did("rest2", tt(squares, spare, xt_parts[:, 1, blocks, :], ALU.subtract))
                between(5)

            def epilogue2(r, between, first=False):
                did = steps(E2_DVE, s_e2d, r)
                v = val2

                def after_act(name):
                    dve.wait_ge(s_e2a, step_value(E2_ACT, r, name))

                dve.wait_ge(s_e2t, r + 1)
                after_act("s_squares")
                did("relu", ts(h_rows, mm_blocks, 0.0, ALU.max))
                did("s_sq", nc.vector.tensor_reduce(v["s_sq"], squares, AX, ALU.add))
                after_act("r_squares")
                did("r_sq", nc.vector.tensor_reduce(v["r_sq"], spare, AX, ALU.add))
                did("floor_s", ts(v["s_sq"], v["s_sq"], MIN_SQ, ALU.max))
                after_act("th")
                did("th_clipped", ts(v["c"], v["th"], MAX_NORM, ALU.min))
                log_argument(did, "s_", v, v["c"])
                after_act("s_log")
                log_result(did, "s_", v)
                did("inv_un", nc.vector.reciprocal(v["iun"], v["un"]))
                did("kappa", tt(v["kappa"], v["atanh"], v["iun"], ALU.mult))
                did("kk", tt(v["kk"], v["kappa"], v["kappa"], ALU.mult))
                did("w_sq", tt(v["w_sq"], v["kk"], v["r_sq"], ALU.mult))
                did("floor_w", ts(v["w_sq"], v["w_sq"], MIN_SQ, ALU.max))
                between(0)
                after_act("tw")
                did("tw_clipped", ts(v["twc"], v["tw"], MAX_NORM, ALU.min))
                did("inv_wn", nc.vector.reciprocal(v["iwn"], v["wn"]))
                did("kt", tt(v["kt"], v["kappa"], v["twc"], ALU.mult))
                did("kappa2", tt(v["k2"], v["kt"], v["iwn"], ALU.mult))
                dve.wait_ge(s_x1in, 16 * (r + 1))
                if not first:
                    dve.wait_ge(s_out, 16 * r)
                did("scaled", tt(x1_rows, h_rows, wide(v["k2"]), ALU.mult))
                did("with_x1", tt(x1_rows, x1_rows, x_rows, ALU.add))
                between(1)
                normalize_1(did, v)
                normalize_2(did, v, after_act, "out")

            def unpack_all(t, p, q0, q1):
                if q1 - q0 == 1:
                    unpack(t, p, q0)
                else:
                    apart(dve)
                    with dve.Fori(q0, q1) as q:
                        unpack(t, p, q)

            y2 = bias_stats[:, 7:8]

            def prepare_weights():
                bs = bias_stats
                scratch = squares[:, 0, :]
                dve.wait_ge(s_const, 48)
                chained(s_bias, 1, nc.vector.tensor_tensor(scratch, hyp_bias, hyp_bias, ALU.mult))
                chained(s_bias, 2, nc.vector.tensor_reduce(bs[:, 0:1], scratch, AX, ALU.add))
                chained(s_bias, 3, nc.vector.tensor_scalar(bs[:, 1:2], bs[:, 0:1], MIN_SQ, None, ALU.max))
                dve.wait_ge(s_bias_act, 2)
                chained(s_bias, 4, nc.vector.tensor_scalar(bs[:, 4:5], bs[:, 3:4], MAX_NORM, None, ALU.min))
                chained(s_bias, 5, nc.vector.reciprocal(bs[:, 5:6], bs[:, 2:3]))
                chained(s_bias, 6, nc.vector.tensor_tensor(bs[:, 6:7], bs[:, 4:5], bs[:, 5:6], ALU.mult))
                chained(s_bias, 7, nc.vector.tensor_scalar(hyp_bias, hyp_bias, bs[:, 6:7], None, ALU.mult))
                chained(s_bias, 8, nc.vector.tensor_tensor(scratch, hyp_bias, hyp_bias, ALU.mult))
                chained(s_bias, 9, nc.vector.tensor_reduce(y2, scratch, AX, ALU.add))

                dve.wait_ge(s_wT, 1)
                assert BETA == 0.5
                chained(s_bias, 10, nc.vector.tensor_tensor(V, weights_ps[:, 0:C], ident[:, :], ALU.add))
                nc.vector.tensor_scalar(V, V, BETA, None, ALU.mult).then_inc(s_prep, 1)
                nc.vector.tensor_copy(W1T, weights_ps[:, C:2 * C]).then_inc(s_prep, 1)

            def panel_with_epilogue1(t, p, first=False, last=False):
                def between(i):
                    if i < 4:
                        unpack_all(t, p, *[(2, 3), (3, 5), (5, 6), (6, 7)][i])
                        if i == 3 and not last:
                            scale_x(t)
                    elif i == (5 if last else 4):
                        unpack_all(t, p, 7, 8)
                unpack_all(t, p, 0, 2)
                epilogue1(t - 1, between, first)

            def panel_with_epilogue2(t, first=False):
                def between(i):
                    unpack_all(t, t - NP, *[(3, 4), (4, 6)][i])
                unpack_all(t, t - NP, 0, 3)
                epilogue2(t - NP - 1, between, first)
                unpack_all(t, t - NP, 6, 8)

            def at_once(i):
                pass

            def binary():
                edge_degrees()
                dve.wait_ge(s_stored, NB)
                unpack(0, 0, 0, first=True)
                for n in range(NP // 2, NP):
                    add_panel(NG - 1, n)
                split_y(0)
                for q in range(1, NQ - 1):
                    split_y(q)
                    unpack(0, 0, q)
                split_y(NQ - 1)
                scale_x(0, first=True)
                unpack(0, 0, NQ - 1)
                prepare_weights()
                panel_with_epilogue1(1, 1, first=True)
                with dve.Fori(2, NP) as t:
                    panel_with_epilogue1(t, t)
                panel_with_epilogue1(NP, 0, last=True)
                panel_with_epilogue2(NP + 1, True)
                with dve.Fori(NP + 2, 2 * NP) as t:
                    panel_with_epilogue2(t)
                epilogue2(NP - 1, at_once)

            def general():
                for n in range(NP // 2, NP):
                    add_panel(NG - 1, n)
                dve.wait_ge(s_added, NG * NP)
                prepare_weights()
                with dve.Fori(0, NB) as r:
                    for c in range(NCH):
                        dve.wait_ge(s_gload, 16 * (r * NCH + c + 1))
                        nc.vector.tensor_reduce(gvals[:, 4 + c:5 + c], gchunk, AX, ALU.add).then_inc(s_gused, 1)
                    dve.wait_ge(s_gused, (r + 1) * NCH)
                    chained(s_gdve, r + 1, nc.vector.tensor_reduce(degree[:, bass.ds(r, 1)], gvals[:, 4:4 + NCH], AX, ALU.add))
                dve.wait_ge(s_gx, 16)
                nc.vector.tensor_copy(gx[:, :, C:C + 1], degree[:, :].unsqueeze(2)).then_inc(s_gdve, 1)
                nc.vector.memset(gx[:, :, C + 1:C + 2], 1.0).then_inc(s_gdve, 1)
                dve.wait_ge(s_gact, 1)
                chained(s_gdve, NB + 3, nc.vector.reciprocal(node_scale, degree_root))
                chained(s_gdve, NB + 4, nc.vector.tensor_scalar(node_scale, node_scale, 1.0 - ALPHA, None, ALU.mult))
                sums = weights_ps[:, 0:XW]
                with dve.Fori(0, NB) as j:
                    n = NB + 4 + 4 * j
                    dve.wait_ge(s_gused, G_SUMS + PB + j * PB)
                    chained(s_gdve, n + 1, nc.vector.reciprocal(gvals[:, 0:1], sums[:, C + 1:C + 2]))
                    chained(s_gdve, n + 2, nc.vector.tensor_tensor(gvals[:, 1:2], sums[:, C:C + 1], gvals[:, 0:1], ALU.mult))
                    dve.wait_ge(s_gact, j + 2)
                    chained(s_gdve, n + 3, nc.vector.reciprocal(gvals[:, 3:4], gvals[:, 2:3]))
                    out_ = gfull[:, bass.ds(j, 1), :].rearrange("p o c -> p (o c)")
                    chained(s_gdve, n + 4, nc.vector.tensor_scalar(out_, sums[:, 0:C], gvals[:, 3:4], 1.0 / TWO, ALU.mult, ALU.mult))

                def panel_y(e, first=False):
                    dve.wait_ge(s_xrows, 16 * (e + 1))
                    apart(dve)
                    with dve.Fori(0, PB) as b:
                        block_x = x_rows[:, bass.ds(b, 1), :].rearrange("p o c -> p (o c)")
                        nc.vector.tensor_scalar(gshare, block_x, degree_root[:, bass.ds(e * PB + b, 1)],
                                                ALPHA / (1.0 - ALPHA), ALU.mult, ALU.mult).then_inc(s_xsc, 1)
                        dve.wait_ge(s_xsc, e * PB + b + 1)
                        dve.wait_ge(s_gmm, (e * PB + b + 1) * NP)
                        chained(s_grow, e * PB + b + 1, nc.vector.tensor_tensor(grow, gshare, weights_ps[:, 0:C], ALU.add))
                    epilogue1(e, at_once, first)

                def panel_xt(e, first=False):
                    with dve.Fori(0, PB) as b:
                        dve.wait_ge(s_gmm, NP * (NB + 1) + (e * PB + b) * NP)
                        nc.vector.tensor_copy(grow, weights_ps[:, 0:C]).then_inc(s_grow, 1)
                    epilogue2(e, at_once, first)

                panel_y(0, True)
                with dve.Fori(1, NP) as e:
                    panel_y(e)
                dve.wait_ge(s_e1a, step_value(E1_ACT, NP - 1, "part2"))
                n = NB + 4 + 4 * NB
                for i in range(NP):
                    sl = slice(i * PB, (i + 1) * PB)
                    chained(s_gdve, n + 2 * i + 1, nc.vector.tensor_tensor(
                        gfull[:, sl, :], xt_parts[:, 2, sl, :], xt_parts[:, 1, sl, :], ALU.add))
                    chained(s_gdve, n + 2 * i + 2, nc.vector.tensor_tensor(
                        gfull[:, sl, :], gfull[:, sl, :], xt_parts[:, 0, sl, :], ALU.add))
                panel_xt(0, True)
                with dve.Fori(1, NP) as e:
                    panel_xt(e)

            with dve.If(not_binary == 0):
                binary()
            with dve.If(not_binary != 0):
                general()


_INS = ["x", "adj", "L0_gnn_W", "L1_gnn_weight", "L1_gnn_bias"]


def kernel(**inputs):
    import numpy as _np
    import concourse.bacc as _bacc
    from concourse import mybir as _mybir
    from concourse.bass_utils import run_bass_kernel_spmd as _run

    nc = _bacc.Bacc("TRN2", target_bir_lowering=False, num_devices=1)
    arrays, args = {}, []
    for name in _INS:
        a = _np.ascontiguousarray(inputs[name])
        arrays[f"in_{name}"] = a
        args.append(nc.dram_tensor(f"in_{name}", a.shape, _mybir.dt.from_np(a.dtype), kind="ExternalInput").ap())
    out = nc.dram_tensor("out_0", (N, C), _mybir.dt.float32, kind="ExternalOutput").ap()
    x1_dram = nc.dram_tensor("x1", (N, C), _mybir.dt.float32, kind="Internal").ap()
    build(nc, *args, out, x1_dram)
    r = _run(nc, [arrays], core_ids=[0])
    return r.results[0]["out_0"]
```
